# Optimizing a Trainium2 kernel written in Bass

```python
import numpy as np
import jax
import jax.numpy as jnp

def _softmax(x, axis=-1):
    return jax.nn.softmax(x, axis=axis)

def _gelu(x):
    return jax.nn.gelu(x, approximate=True)

def _silu(x):
    return jax.nn.silu(x)

def _sigmoid(x):
    return jax.nn.sigmoid(x)

def _layernorm(x, axis=-1, eps=1e-05):
    m = jnp.mean(x, axis=axis, keepdims=True)
    v = jnp.var(x, axis=axis, keepdims=True)
    return (x - m) / jnp.sqrt(v + eps)

def _scatter_add(tgt, idx, src, axis=0):
    return tgt.at[idx].add(src)

def _segment_sum(src, seg, n):
    return jax.ops.segment_sum(src, seg, n)
kernel_name = 'mk_adaln_ffn_d1_seqx_r8_919c57'

def setup_inputs(seed: int=0):
    np.random.seed(seed)
    _w = jnp.asarray

    def _rec_inputs():
        import jax
        import jax.numpy as jnp
        _rk = jax.random.key(seed)
        x = -0.0003929 + 0.9999 * jax.random.normal(jax.random.fold_in(_rk, 1), (16, 128, 128), jnp.float32)
        _lenS = 128 - jax.random.randint(jax.random.fold_in(_rk, 7), (16,), 0, max(1, 128 // 4) + 1, jnp.int32)
        _lenS2 = 128 - jax.random.randint(jax.random.fold_in(_rk, 8), (16,), 0, max(1, 128 // 4) + 1, jnp.int32)
        fside_Bx1x1024x16_0 = 0.00222621 + 0.99962 * jax.random.normal(jax.random.fold_in(_rk, 11), (16, 1, 128, 16), jnp.float32)
        cond_1024 = -0.00745576 + 0.997402 * jax.random.normal(jax.random.fold_in(_rk, 12), (16, 128), jnp.float32)
        return (x, fside_Bx1x1024x16_0, cond_1024)
    x, fside_Bx1x1024x16_0, cond_1024 = _rec_inputs()

    def _L0_cond_setup():
        import jax, jax.numpy as jnp
        import numpy as np
        B, F_, IN, OUT, R = (32, 64, 128, 128, 16)
        key = jax.random.key(seed)
        ks = jax.random.split(key, 6)
        x = jax.random.normal(ks[0], (B, F_, IN), dtype=jnp.float32)
        u = jax.random.normal(ks[1], (B, 1, OUT, R), dtype=jnp.float32)
        v = jax.random.normal(ks[2], (B, 1, IN, R), dtype=jnp.float32)
        b = jax.random.normal(ks[3], (B, 1, OUT), dtype=jnp.float32)
        lim = 1.0 / np.sqrt(IN)
        W = jax.random.uniform(ks[4], (OUT, IN), minval=-lim, maxval=lim, dtype=jnp.float32)
        fc_bias = jax.random.uniform(ks[5], (OUT,), minval=-lim, maxval=lim, dtype=jnp.float32)
        return {'x': x, 'u': u, 'v': v, 'b': b, 'W': W, 'fc_bias': fc_bias}
    _L0_cond_all = _L0_cond_setup()
    _L0_cond_in = {k: v for k, v in _L0_cond_all.items() if k in ('W', 'fc_bias')}
    del _L0_cond_all

    def _L0_ffn_setup():
        import jax, jax.numpy as jnp
        import numpy as np
        import math
        E = 16
        TOP_K = 2
        D = 128
        F = 512
        SH = 256
        key = jax.random.key(seed)
        ks = jax.random.split(key, 10)
        s = lambda k, shape, fan: jax.random.normal(k, shape, jnp.float32) / np.sqrt(fan)
        return {'x': jax.random.normal(ks[0], (32, 32, D), jnp.float32), 'gate_w': s(ks[1], (E, D), D), 'up_w': s(ks[2], (E, F, D), D), 'up_b': s(ks[3], (E, F), D), 'gw': s(ks[4], (E, F, D), D), 'gb': s(ks[5], (E, F), D), 'down_w': s(ks[6], (E, D, F), F), 'down_b': s(ks[7], (E, D), F), 'sh_gate_w': s(ks[8], (SH, D), D), 'sh_up_w': s(ks[9], (SH, D), D), 'sh_down_w': s(jax.random.fold_in(key, 11), (D, SH), SH)}
    _L0_ffn_all = _L0_ffn_setup()
    _L0_ffn_in = {k: v for k, v in _L0_ffn_all.items() if k in ('gate_w', 'up_w', 'up_b', 'gw', 'gb', 'down_w', 'down_b', 'sh_gate_w', 'sh_up_w', 'sh_down_w')}
    del _L0_ffn_all
    return {'x': x, 'fside_Bx1x1024x16_0': fside_Bx1x1024x16_0, 'cond_1024': cond_1024, 'L0_cond_W': _L0_cond_in['W'], 'L0_cond_fc_bias': _L0_cond_in['fc_bias'], 'L0_ffn_gate_w': _L0_ffn_in['gate_w'], 'L0_ffn_up_w': _L0_ffn_in['up_w'], 'L0_ffn_up_b': _L0_ffn_in['up_b'], 'L0_ffn_gw': _L0_ffn_in['gw'], 'L0_ffn_gb': _L0_ffn_in['gb'], 'L0_ffn_down_w': _L0_ffn_in['down_w'], 'L0_ffn_down_b': _L0_ffn_in['down_b'], 'L0_ffn_sh_gate_w': _L0_ffn_in['sh_gate_w'], 'L0_ffn_sh_up_w': _L0_ffn_in['sh_up_w'], 'L0_ffn_sh_down_w': _L0_ffn_in['sh_down_w']}

def reference(x, fside_Bx1x1024x16_0, cond_1024, L0_cond_W, L0_cond_fc_bias, L0_ffn_gate_w, L0_ffn_up_w, L0_ffn_up_b, L0_ffn_gw, L0_ffn_gb, L0_ffn_down_w, L0_ffn_down_b, L0_ffn_sh_gate_w, L0_ffn_sh_up_w, L0_ffn_sh_down_w):
    import jax
    import jax.numpy as jnp

    def _L0_cond_ref(x, u, v, b, W, fc_bias):
        import jax, jax.numpy as jnp
        import numpy as np
        B, F_, IN, OUT, R = (32, 64, 128, 128, 16)
        inch = x.shape[-1]
        r = v.shape[-1]
        z1 = jnp.einsum('bfi,bir->bfr', x, v[:, 0]) / inch
        z = jnp.einsum('bfr,bor->bfo', z1, u[:, 0]) / r
        y = jnp.einsum('bfi,oi->bfo', x, W) + fc_bias + z + b
        return jax.nn.gelu(y, approximate=False)

    def _L0_ffn_ref(x, gate_w, up_w, up_b, gw, gb, down_w, down_b, sh_gate_w, sh_up_w, sh_down_w):
        import jax, jax.numpy as jnp
        import numpy as np
        import math
        E = 16
        TOP_K = 2
        D = 128
        F = 512
        SH = 256
        B, S, Dm = x.shape
        h = x.reshape(-1, Dm)
        T = h.shape[0]
        scores = jax.nn.sigmoid(h @ gate_w.T)
        cap = math.ceil(T / E * TOP_K)
        topk_score, topk_ids = jax.lax.top_k(scores.T, cap)
        xin = h[topk_ids]
        up = jnp.einsum('ecd,efd->ecf', xin, up_w) + up_b[:, None, :]
        g = jnp.einsum('ecd,efd->ecf', xin, gw) + gb[:, None, :]
        eo = jax.nn.silu(g) * up
        eo = jnp.einsum('ecf,edf->ecd', eo, down_w) + down_b[:, None, :]
        flat = (eo * topk_score[..., None]).reshape(-1, Dm)
        out = jnp.zeros_like(h).at[topk_ids.reshape(-1)].add(flat)
        out = out.reshape(B, S, Dm)
        shared = jax.nn.silu(jnp.einsum('bsd,fd->bsf', x, sh_gate_w)) * jnp.einsum('bsd,fd->bsf', x, sh_up_w)
        shared = jnp.einsum('bsf,df->bsd', shared, sh_down_w)
        return out + shared
    x = x + _L0_ffn_ref(_L0_cond_ref(x, fside_Bx1x1024x16_0, fside_Bx1x1024x16_0, cond_1024[:, None, :], L0_cond_W, L0_cond_fc_bias), L0_ffn_gate_w, L0_ffn_up_w, L0_ffn_up_b, L0_ffn_gw, L0_ffn_gb, L0_ffn_down_w, L0_ffn_down_b, L0_ffn_sh_gate_w, L0_ffn_sh_up_w, L0_ffn_sh_down_w)
    return x

_drawn_inputs = setup_inputs


def setup_inputs(seed=0):
    import zlib

    import numpy as np

    out = dict(_drawn_inputs(seed))
    spreads = {}
    factors = {}
    for name, (base, spread) in spreads.items():
        noise = np.random.default_rng([zlib.crc32(name.encode()), seed]).standard_normal(out[name].shape)
        drawn = base * np.exp(spread * noise) if base else spread * noise
        out[name] = jnp.asarray(drawn.astype(out[name].dtype))
    for name, factor in factors.items():
        out[name] = (out[name] * factor).astype(out[name].dtype)
    return out
```

```python
from contextlib import ExitStack

import concourse.bass as bass
from concourse import mybir

ALU = mybir.AluOpType
ACT = mybir.ActivationFunctionType
AX_X = mybir.AxisListType.X
F32 = mybir.dt.float32
BF16 = mybir.dt.bfloat16
I32 = mybir.dt.int32

P = 128
B = 16
T = B * P
R = 16
E = 16
CAP = T * 2 // E
CT = CAP // P
F = 512
FC = F // P
SH = 256
SC = SH // P
K = P // E
CH = T // K
HB = CH // P
ROW = P + E
STEPS = 15

C_WT, C_COND, C_FCB, C_GATE, C_ID, C_J, C_Q = 0, 128, 144, 145, 385, 513, 514
C_N = C_Q + STEPS
GATE_AT = P - E
B_ONES, B_LOW, B_IOTA, B_BLK = 0, P, 2 * P, 2 * P + P * B
B_N = B_BLK + E * B
S_G, S_U, S_D = 0, SH, 2 * SH
S_N = 3 * SH
G_G, G_U, G_GB, G_UB = 0, F, 2 * F, 2 * F + FC
G_N = 2 * F + 2 * FC


def moe_program(nc, xT, x, fsT, cf, cb, bits, shw, wgu, wd, down_b, out):
    ctx = ExitStack()
    with ctx:
        def sb(name, shape, dt=F32):
            return ctx.enter_context(nc.sbuf_tensor(name, shape, dt))

        def sem(name):
            return ctx.enter_context(nc.semaphore(name))

        table = nc.dram_tensor("h_and_scores", (T, ROW), F32, kind="Internal").ap()

        xT_sb = sb("xT_sb", [P, B, P])
        x_sb = sb("x_sb", [P, B, P])
        fsT_sb = sb("fsT_sb", [R, B, P])
        cf_sb = sb("cf_sb", [P, C_N])
        cb_sb = sb("cb_sb", [P, B_N], BF16)
        bits_sb = sb("bits_sb", [P, STEPS + 1, 3], I32)
        sh_sb = sb("sh_sb", [P, S_N])
        db_sb = sb("db_sb", [P, E, P])
        wgu_sb = [sb(f"wgu{i}", [P, G_N]) for i in range(2)]
        wd_sb = [sb(f"wd{i}", [P, FC, P]) for i in range(2)]

        biasT = sb("biasT", [P, B])
        weff = sb("weff", [P, B, P])
        hT = sb("hT", [P, T])
        hrow = sb("hrow", [P, B, ROW])
        score = sb("score", [P, CH])

        cand = sb("cand", [P, 3], I32)
        base = sb("base", [P, 3], I32)
        thr = sb("thr", [P, 1], I32)
        found = sb("found", [P, 1], I32)
        passed = sb("passed", [P, 3])
        hits = sb("hits", [P, 3, CH])
        cnt = sb("cnt", [P, 3], BF16)
        rank_cnt = sb("rank_cnt", [P, 3], BF16)
        offs = sb("offs", [P, 2])
        above = sb("above", [P, CH])
        equal = sb("equal", [P, CH])
        zeros = sb("zeros", [P, CH])
        rank_a = sb("rank_a", [P, CH])
        rank_b = sb("rank_b", [P, CH])
        slot = sb("slot", [P, CH])
        second = sb("second", [P, E, B])
        row_of = sb("row_of", [P, E, B], BF16)
        parts = sb("parts", [P, CT, 2, E, B], BF16)

        sh_silu = sb("sh_silu", [P, SH])
        sh_up = sb("sh_up", [P, SH])
        sh_act = sb("sh_act", [P, SH])
        sh_y = sb("sh_y", [P, P])
        first = sb("first", [P, B, P])

        onehot = [sb(f"onehot{i}", [P, P, B], BF16) for i in range(2)]
        idx_all = sb("idx_all", [P, E, CT], I32)
        idx_g = [sb(f"idx_g{i}", [P, CT], I32) for i in range(2)]
        idx_s = [sb(f"idx_s{i}", [P, CT], I32) for i in range(2)]
        rows = [sb(f"rows{i}", [P, CT, ROW]) for i in range(2)]
        weight = sb("weight", [P, E, CT])
        xinT = [sb(f"xinT{i}", [P, CAP]) for i in range(2)]
        silu = sb("silu", [P, FC, CAP])
        act_sb = [sb(f"act{i}", [P, FC, CAP]) for i in range(2)]
        y_raw = sb("y_raw", [P, CT, P])
        y_sb = [sb(f"y{i}", [P, CT, P]) for i in range(2)]

        bank = [ctx.enter_context(nc.psum_tensor(f"bank{i}", [P, 512], F32)) for i in range(8)]

        WT = cf_sb[:, C_WT:C_WT + P]
        ident = cf_sb[:, C_ID:C_ID + P]
        token = cf_sb[:, C_J:C_J + 1]
        ones = cb_sb[:, B_ONES:B_ONES + P]
        lower = cb_sb[:, B_LOW:B_LOW + P]
        iota = cb_sb[:, B_IOTA:B_IOTA + P * B].rearrange("p (m b) -> p m b", b=B)
        block_at = cb_sb[:, B_BLK:B_BLK + E * B].rearrange("p (e b) -> p e b", b=B)

        ld_fs, ld_cf, ld_cb, ld_bits = sem("ld_fs"), sem("ld_cf"), sem("ld_cb"), sem("ld_bits")
        ld_x = [sem(f"ld_x{g}") for g in range(4)]
        ld_sh, ld_xrow, ld_db = sem("ld_sh"), sem("ld_xrow"), sem("ld_db")
        ld_wgu = [sem(f"ld_wgu{i}") for i in range(2)]
        ld_wd = [sem(f"ld_wd{i}") for i in range(2)]
        bias_ready, lowrank_ready, weff_ready = sem("bias_ready"), sem("lowrank_ready"), sem("weff_ready")
        y_ready, h_ready, hrow_T, hrow_ready = sem("y_ready"), sem("h_ready"), sem("hrow_T"), sem("hrow_ready")
        logits_ready, score_ready, scoreT, hscore_ready = (
            sem("logits_ready"), sem("score_ready"), sem("scoreT"), sem("hscore_ready"))
        counted, summed, step_done = sem("counted"), sem("summed"), sem("step_done")
        sh_gu, sh_silu_ready, sh_up_ready, sh_act_ready, sh_down, sh_y_ready, first_ready = (
            sem("sh_gu"), sem("sh_silu_ready"), sem("sh_up_ready"), sem("sh_act_ready"), sem("sh_down"),
            sem("sh_y_ready"), sem("first_ready"))
        rank_counted, offs_ready, slot_ready, slotT, chain = (
            sem("rank_counted"), sem("offs_ready"), sem("slot_ready"), sem("slotT"), sem("chain"))
        parts_ready, pool_turn = sem("parts_ready"), sem("pool_turn")
        table_done = [sem(f"table_done{i}") for i in range(2)]
        first_done = [sem(f"first_done{i}") for i in range(2)]
        onehot_ready, idx_summed, idx_ready = sem("onehot_ready"), sem("idx_summed"), sem("idx_ready")
        gathered = [sem(f"gathered{i}") for i in range(2)]
        scattered = [sem(f"scattered{i}") for i in range(2)]
        xin_T, xin_ready = sem("xin_T"), sem("xin_ready")
        gu_ready, silu_ready, act_ready = sem("gu_ready"), sem("silu_ready"), sem("act_ready")
        down_ready, y_read, y_done = sem("down_ready"), sem("y_read"), sem("y_done")

        def loads(s, e):
            return e // 2 * s + s

        PAIRS = (E - 4) // 2

        block = ctx.enter_context(nc.Block())

        @block.sync
        def _(sp):
            sp.dma_start(fsT_sb[:], fsT).then_inc(ld_fs, 16)
            sp.dma_start(cf_sb[:], cf).then_inc(ld_cf, 16)
            for g in range(4):
                sp.dma_start(xT_sb[:, 4 * g:4 * g + 4, :], xT[:, 4 * g:4 * g + 4, :]).then_inc(ld_x[g], 16)
            sp.dma_start(sh_sb[:], shw).then_inc(ld_sh, 16)
            sp.dma_start(x_sb[:], x).then_inc(ld_xrow, 16)
            for e in range(2):
                sp.dma_start(wgu_sb[e][:], wgu[e]).then_inc(ld_wgu[e], 16)
                sp.dma_start(wd_sb[e][:], wd[e]).then_inc(ld_wd[e], 16)
            sp.wait_ge(hrow_ready, 4)
            sp.wait_ge(hscore_ready, 1)
            trows = table.rearrange("(b p) c -> p b c", p=P)
            for n in range(2):
                sp.dma_start(trows[:, 8 * n:8 * n + 8, :], hrow[:, 8 * n:8 * n + 8, :]).then_inc(table_done[n], 16)
            orows = out.rearrange("b p c -> p b c")
            for n in range(2):
                sp.wait_ge(first_ready, 8 * n + 8)
                sp.dma_start(orows[:, 8 * n:8 * n + 8, :], first[:, 8 * n:8 * n + 8, :]).then_inc(first_done[n], 16)

            def load_gu(e, p):
                sp.wait_ge(act_ready, e * FC - FC)
                sp.dma_start(wgu_sb[p][:], wgu[bass.ds(e, 1)].rearrange("o p c -> (o p) c")).then_inc(ld_wgu[p], 16)

            def load_d(e, p):
                sp.wait_ge(down_ready, e - 1)
                sp.dma_start(wd_sb[p][:], wd[bass.ds(e, 1)].rearrange("o p c d -> (o p) c d")).then_inc(ld_wd[p], 16)

            with sp.Fori(0, (E - 2) // 2) as i:
                for u in range(2):
                    load_gu(i * 2 + (2 + u), u)
                    load_d(i * 2 + (2 + u), u)
            for s in scattered:
                sp.wait_ge(s, 16 * CT * E // 2)

        @block.tensor
        def _(pe):
            pe.wait_ge(ld_fs, 16)
            for b in range(B):
                mm = pe.matmul(bank[b // 4][:, b % 4 * P:(b % 4 + 1) * P], fsT_sb[:, b, :], fsT_sb[:, b, :],
                               start=True, stop=True)
                if b % 4 == 3:
                    mm.then_inc(lowrank_ready, 1)
            for b in range(B):
                if b % 4 == 0:
                    pe.wait_ge(weff_ready, b // 4 + 1)
                    pe.wait_ge(ld_x[b // 4], 16)
                mm = pe.matmul(bank[4 + b // 4][:, b % 4 * P:(b % 4 + 1) * P], weff[:, b, :], xT_sb[:, b, :],
                               start=True, stop=True)
                if b % 4 == 3:
                    mm.then_inc(y_ready, 1)
            pe.wait_ge(ld_cf, 16)
            for g in range(4):
                for b in range(4 * g, 4 * g + 4):
                    pe.wait_ge(h_ready, max(b + 1, 4))
                    tr = pe.transpose(bank[g][:, b % 4 * P:(b % 4 + 1) * P], hT[:, b * P:(b + 1) * P], ident)
                    if b % HB == HB - 1:
                        k = b // HB
                        at = C_GATE + GATE_AT - E * k
                        mm = pe.matmul(bank[4][:, 0:CH], cf_sb[:, at:at + P], hT[:, k * CH:(k + 1) * CH],
                                       start=(k == 0), stop=(k == K - 1))
                tr.then_inc(hrow_T, 1)
            mm.then_inc(logits_ready, 1)
            pe.wait_ge(score_ready, 1)
            for h in range(HB):
                tr = pe.transpose(bank[5][:, h * P:(h + 1) * P], score[:, h * P:(h + 1) * P], ident)
            tr.then_inc(scoreT, 1)

            def sum_counts(n):
                pe.wait_ge(counted, n + 1)
                pe.matmul(bank[0][:, 0:3], ones, cnt[:], start=True, stop=True).then_inc(summed, 1)

            def shared_in(t, ahead):
                if ahead:
                    pe.wait_ge(sh_up_ready, t)
                for c in range(2 * SC):
                    mm = pe.matmul(bank[1][:, c * P:(c + 1) * P], sh_sb[:, c * P:(c + 1) * P],
                                   hT[:, bass.ds(t * P, P)], start=True, stop=True)
                mm.then_inc(sh_gu, 1)

            def shared_out(t, ahead):
                pe.wait_ge(sh_act_ready, t + 1)
                if ahead:
                    pe.wait_ge(sh_y_ready, t)
                for c in range(SC):
                    mm = pe.matmul(bank[2][:, 0:P], sh_act[:, c * P:(c + 1) * P],
                                   sh_sb[:, S_D + c * P:S_D + (c + 1) * P], start=(c == 0), stop=(c == SC - 1))
                mm.then_inc(sh_down, 1)

            pe.wait_ge(ld_cb, 16)
            pe.wait_ge(ld_sh, 16)
            pe.wait_ge(hrow_ready, 4)
            shared_in(0, False)
            sum_counts(0)
            shared_in(1, True)
            shared_out(0, False)
            sum_counts(1)
            with pe.Fori(2, STEPS) as i:
                shared_in(i, True)
                shared_out(i - 1, True)
                sum_counts(i)
            shared_in(B - 1, True)
            shared_out(B - 2, True)
            pe.wait_ge(rank_counted, 1)
            pe.matmul(bank[0][:, 8:10], lower, rank_cnt[:, 1:3], start=True, stop=False)
            pe.matmul(bank[0][:, 8:10], ones, rank_cnt[:, 0:2], start=False, stop=True).then_inc(offs_ready, 1)
            shared_out(B - 1, True)
            pe.wait_ge(slot_ready, 1)
            for h in range(HB):
                tr = pe.transpose(bank[3][:, h * P:(h + 1) * P], slot[:, h * P:(h + 1) * P], ident)
            tr.then_inc(slotT, 1)

            def sum_indices(e, p, ahead):
                pe.wait_ge(onehot_ready, e + 1)
                if ahead:
                    pe.wait_ge(idx_ready, e)
                for b in range(B):
                    rhs = parts[:, :, :, bass.ds(e, 1), b].rearrange("p n q o -> p (n q o)")
                    mm = pe.matmul(bank[0][:, 0:2 * CT], onehot[p][:, :, b], rhs, start=(b == 0), stop=(b == B - 1))
                mm.then_inc(idx_summed, 1)

            def transpose_rows(e, p, ahead):
                pe.wait_ge(gathered[p], loads(16 * CT, e))
                if ahead:
                    pe.wait_ge(xin_ready, e)
                for c in range(CT):
                    tr = pe.transpose(bank[3][:, c * P:(c + 1) * P], rows[p][:, c, 0:P], ident)
                tr.then_inc(xin_T, 1)

            def gate_up(e, p, ahead):
                pe.wait_ge(xin_ready, e + 1)
                pe.wait_ge(ld_wgu[p], loads(16, e))
                for f in range(FC):
                    if ahead:
                        pe.wait_ge(act_ready, e * FC + (f + 1 - FC))
                    pe.matmul(bank[4 + f][:, 0:CAP], wgu_sb[p][:, G_G + f * P:G_G + (f + 1) * P], xinT[p][:],
                              start=True, stop=True)
                    pe.matmul(bank[4 + f][:, CAP:2 * CAP], wgu_sb[p][:, G_U + f * P:G_U + (f + 1) * P],
                              xinT[p][:], start=True, stop=True).then_inc(gu_ready, 1)

            def down(e, p, ahead):
                pe.wait_ge(act_ready, e * FC + FC)
                pe.wait_ge(ld_wd[p], loads(16, e))
                if ahead:
                    pe.wait_ge(y_read, e)
                for c in range(CT):
                    for f in range(FC):
                        mm = pe.matmul(bank[2][:, c * P:(c + 1) * P], act_sb[p][:, f, c * P:(c + 1) * P],
                                       wd_sb[p][:, f, :], start=(f == 0), stop=(f == FC - 1))
                mm.then_inc(down_ready, 1)

            def expert(e, p):
                transpose_rows(e + 1, 1 - p, True)
                gate_up(e, p, True)
                sum_indices(e + 3, 1 - p, True)
                down(e - 1, 1 - p, True)

            pe.wait_ge(parts_ready, 1)
            for e in range(3):
                sum_indices(e, e % 2, e > 0)
            transpose_rows(0, 0, False)
            transpose_rows(1, 1, True)
            gate_up(0, 0, False)
            sum_indices(3, 1, True)
            pe.wait_ge(sh_y_ready, B)
            transpose_rows(2, 0, True)
            gate_up(1, 1, True)
            sum_indices(4, 0, True)
            down(0, 0, False)
            with pe.Fori(0, PAIRS - 1) as i:
                for u in range(2):
                    expert(i * 2 + (2 + u), u)
            for e in range(2 * PAIRS, E):
                if e + 1 < E:
                    transpose_rows(e + 1, 1 - e % 2, True)
                gate_up(e, e % 2, True)
                if e + 3 < E:
                    sum_indices(e + 3, 1 - e % 2, True)
                down(e - 1, 1 - e % 2, True)
            down(E - 1, 1, True)

        @block.scalar
        def _(act):
            act.dma_start(cb_sb[:], cb).then_inc(ld_cb, 16)
            act.dma_start(bits_sb[:], bits).then_inc(ld_bits, 16)
            act.dma_start(db_sb[:], down_b.partition_broadcast(P)).then_inc(ld_db, 16)
            act.wait_ge(bias_ready, 1)
            for b in range(B):
                if b % 4 == 0:
                    act.wait_ge(y_ready, b // 4 + 1)
                act.activation(hT[:, b * P:(b + 1) * P], bank[4 + b // 4][:, b % 4 * P:(b % 4 + 1) * P],
                               ACT.Gelu, bias=biasT[:, b:b + 1]).then_inc(h_ready, 1)
            act.wait_ge(logits_ready, 1)
            act.activation(score[:], bank[4][:, 0:CH], ACT.Sigmoid).then_inc(score_ready, 1)
            act.wait_ge(scoreT, 1)
            act.activation(hrow[:, :, P:ROW].rearrange("p (k h) e -> p h k e", h=HB),
                           bank[5][:, 0:CH].rearrange("p (h k e) -> p h k e", h=HB, k=K), ACT.Copy
                           ).then_inc(hscore_ready, 1)

            def shared_read(t, ahead):
                act.wait_ge(sh_gu, t + 1)
                if ahead:
                    act.wait_ge(sh_act_ready, t)
                act.activation(sh_silu[:], bank[1][:, 0:SH], ACT.Silu).then_inc(sh_silu_ready, 1)
                act.activation(sh_up[:], bank[1][:, SH:2 * SH], ACT.Copy).then_inc(sh_up_ready, 1)

            def shared_y(t, ahead):
                act.wait_ge(sh_down, t + 1)
                if ahead:
                    act.wait_ge(first_ready, t)
                act.activation(sh_y[:], bank[2][:, 0:P], ACT.Copy).then_inc(sh_y_ready, 1)

            shared_read(0, False)
            shared_read(1, True)
            shared_y(0, False)
            with act.Fori(2, B) as i:
                shared_read(i, True)
                shared_y(i - 1, True)
            shared_y(B - 1, True)

            def read_rows(e, p, ahead):
                act.wait_ge(gathered[p], loads(16 * CT, e))
                act.activation(weight[:, bass.ds(e, 1), :].rearrange("p o c -> p (o c)"),
                               rows[p][:, :, bass.ds(P + e, 1)].rearrange("p c o -> p (c o)"), ACT.Copy)
                act.wait_ge(xin_T, e + 1)
                if ahead:
                    act.wait_ge(gu_ready, e * FC - FC)
                act.activation(xinT[p][:], bank[3][:, 0:CAP], ACT.Copy).then_inc(xin_ready, 1)

            def silus(e, p, ahead):
                for f in range(FC):
                    act.wait_ge(gu_ready, e * FC + (f + 1))
                    if ahead:
                        act.wait_ge(act_ready, e * FC + (f + 1 - FC))
                    act.activation(silu[:, f, :], bank[4 + f][:, 0:CAP], ACT.Silu,
                                   bias=wgu_sb[p][:, G_GB + f:G_GB + f + 1]).then_inc(silu_ready, 1)

            act.wait_ge(ld_wgu[0], 16)
            read_rows(0, 0, False)
            read_rows(1, 1, False)
            silus(0, 0, False)
            act.wait_ge(ld_wgu[1], 16)
            with act.Fori(0, (E - 2) // 2) as i:
                for u in range(2):
                    e = i * 2 + (1 + u)
                    read_rows(e + 1, u, True)
                    act.wait_ge(ld_wgu[1 - u], 16 * (i + (1 + u)) if u == 0 else 16 * (i + 2))
                    silus(e, 1 - u, True)
            silus(E - 1, 1, True)

        @block.gpsimd
        def _(pool):
            pool.wait_ge(ld_xrow, 16)

            def shared_mul(t, ahead):
                pool.wait_ge(sh_up_ready, t + 1)
                if ahead:
                    pool.wait_ge(sh_down, t)
                pool.tensor_tensor(sh_act[:], sh_silu[:], sh_up[:], ALU.mult).then_inc(sh_act_ready, 1)

            def add_x(t):
                pool.wait_ge(sh_y_ready, t + 1)
                pool.tensor_tensor(first[:, bass.ds(t, 1), :].rearrange("p o c -> p (o c)"), sh_y[:],
                                   x_sb[:, bass.ds(t, 1), :].rearrange("p o c -> p (o c)"), ALU.add
                                   ).then_inc(first_ready, 1)

            shared_mul(0, False)
            with pool.Fori(1, B) as i:
                shared_mul(i, True)
                add_x(i - 1)
            add_x(B - 1)

            def gather(e, p, ahead):
                pool.wait_ge(idx_ready, e + 1)
                if ahead:
                    pool.wait_ge(xin_ready, e - 1)
                pool.sem_inc(pool_turn, 1)
                for c in range(CT):
                    pool.indirect_dma_start(rows[p][:, c, :], None, table,
                                            bass.IndirectOffsetOnAxis(ap=idx_g[p][:, c:c + 1], axis=0)
                                            ).then_inc(gathered[p], 16)

            def scatter(e, p, ahead):
                pool.wait_ge(y_done, e + 1)
                if ahead:
                    pool.wait_ge(scattered[1 - p], loads(16 * CT, e - 1))
                pool.sem_inc(pool_turn, 1)
                for c in range(CT):
                    pool.indirect_dma_start(out.rearrange("b p c -> (b p) c"),
                                            bass.IndirectOffsetOnAxis(ap=idx_s[p][:, c:c + 1], axis=0),
                                            y_sb[p][:, c, :], None, compute_op=ALU.add
                                            ).then_inc(scattered[p], 16)

            for n in range(2):
                pool.wait_ge(table_done[n], 16)
            gather(0, 0, False)
            gather(1, 1, False)
            gather(2, 0, True)
            gather(3, 1, True)
            for n in range(2):
                pool.wait_ge(first_done[n], 16)
            scatter(0, 0, False)
            with pool.Fori(0, (E - 4) // 2) as i:
                for u in range(2):
                    gather(i * 2 + (4 + u), u, True)
                    scatter(i * 2 + (1 + u), 1 - u, True)
            for e in range(E - 3, E):
                scatter(e, e % 2, True)

        @block.vector
        def _(dve):
            linked = [0]

            def link(ins):
                linked[0] += 1
                ins.then_inc(chain, 1)
                dve.wait_ge(chain, linked[0])

            dve.memset(zeros[:], 0.0)
            dve.memset(rank_cnt[:], 0.0)
            dve.memset(thr[:], 0)
            dve.wait_ge(ld_cf, 16)
            dve.tensor_scalar(biasT[:], cf_sb[:, C_COND:C_COND + B], cf_sb[:, C_FCB:C_FCB + 1], None, ALU.add
                              ).then_inc(bias_ready, 1)
            for g in range(4):
                dve.wait_ge(lowrank_ready, g + 1)
                dve.scalar_tensor_tensor(weff[:, 4 * g:4 * g + 4, :],
                                         bank[g][:, :].rearrange("p (b o) -> p b o", b=4), 1.0 / (P * R),
                                         WT[:, None, :].broadcast_to([P, 4, P]), ALU.mult, ALU.add
                                         ).then_inc(weff_ready, 1)
            for g in range(4):
                dve.wait_ge(hrow_T, g + 1)
                dve.tensor_copy(hrow[:, 4 * g:4 * g + 4, 0:P], bank[g][:, :].rearrange("p (b o) -> p b o", b=4)
                                ).then_inc(hrow_ready, 1)
            dve.wait_ge(ld_bits, 16)
            link(dve.tensor_copy(cand[:], bits_sb[:, 0, :]))
            dve.wait_ge(score_ready, 1)
            dve.wait_ge(ld_cb, 16)
            n0 = linked[0]
            with dve.Fori(0, STEPS) as i:
                def step_link(ins, j):
                    ins.then_inc(step_done, 1)
                    dve.wait_ge(step_done, i * 4 + j)

                for j in range(3):
                    c = dve.tensor_scalar(hits[:, j, :], score[:], cand[:, j:j + 1].bitcast(F32), None, ALU.is_ge,
                                          ALU.add, accum_out=cnt[:, j:j + 1])
                c.then_inc(counted, 1)
                dve.tensor_tensor(base[:], thr[:].broadcast_to([P, 3]),
                                  bits_sb[:, bass.ds(i + 1, 1), :].rearrange("p o c -> p (o c)"),
                                  ALU.bitwise_or)
                dve.wait_ge(summed, i + 1)
                step_link(dve.tensor_scalar(passed[:], bank[0][:, 0:3], float(CAP),
                                            cf_sb[:, bass.ds(i + C_Q, 1)], ALU.is_ge, ALU.mult), 1)
                with nc.allow_low_precision(reason="integers below 2^30 with two set bits"):
                    step_link(dve.tensor_reduce(found[:], passed[:], AX_X, ALU.add), 2)
                step_link(dve.tensor_tensor(cand[:], base[:], found[:].broadcast_to([P, 3]), ALU.bitwise_or), 3)
                step_link(dve.tensor_tensor(thr[:], thr[:], found[:], ALU.bitwise_or), 4)
            thr_f = thr[:].bitcast(F32)
            dve.tensor_scalar(above[:], score[:], thr_f, None, ALU.is_gt, ALU.add, accum_out=rank_cnt[:, 1:2])
            dve.tensor_scalar(equal[:], score[:], thr_f, None, ALU.is_equal, ALU.add,
                              accum_out=rank_cnt[:, 2:3]).then_inc(rank_counted, 1)
            dve.wait_ge(offs_ready, 1)
            link(dve.tensor_copy(offs[:], bank[0][:, 8:10]))
            dve.tensor_tensor_scan(rank_a[:], above[:], zeros[:], offs[:, 0:1], ALU.add, ALU.add)
            link(dve.tensor_tensor_scan(rank_b[:], equal[:], zeros[:], offs[:, 1:2], ALU.add, ALU.add))
            dve.tensor_tensor(rank_a[:], rank_a[:], above[:], ALU.mult)
            link(dve.tensor_tensor(rank_b[:], rank_b[:], equal[:], ALU.mult))
            dve.tensor_tensor(slot[:], rank_a[:], rank_b[:], ALU.add).then_inc(slot_ready, 1)
            dve.wait_ge(slotT, 1)
            at = bank[3][:, 0:CH].rearrange("p (b e) -> p e b", e=E)

            link(dve.tensor_scalar(second[:], at, float(P), None, ALU.is_gt))
            dve.scalar_tensor_tensor(row_of[:], second[:], -float(P), at, ALU.mult, ALU.add)
            for n, op in enumerate((ALU.is_le, ALU.is_gt)):
                dve.tensor_scalar(parts[:, n, 0], at, float(P), token, op, ALU.mult)
                last = dve.scalar_tensor_tensor(parts[:, n, 1], at, float(P), block_at, op, ALU.mult)
            link(last)
            dve.engine_nop().then_inc(parts_ready, 1)

            def one_hot(e, p, ahead):
                if ahead:
                    dve.wait_ge(idx_summed, e - 1)
                dve.tensor_tensor(onehot[p][:], iota, row_of[:, bass.ds(e, 1), :].broadcast_to([P, P, B]),
                                  ALU.is_equal).then_inc(onehot_ready, 1)

            def indices(e, p, ahead):
                dve.wait_ge(idx_summed, e + 1)
                if ahead:
                    dve.wait_ge(gathered[p], loads(16 * CT, e - 2))
                pair = bank[0][:, 0:2 * CT].rearrange("p (n q) -> p n q", q=2)
                with nc.allow_low_precision(reason="token numbers"):
                    dve.tensor_reduce(idx_all[:, bass.ds(e, 1), :].rearrange("p o c -> p (o c)"), pair, AX_X,
                                      ALU.add)
                    dve.tensor_reduce(idx_g[p][:], pair, AX_X, ALU.add).then_inc(idx_ready, 1)

            def gated(e, p, ahead):
                if ahead:
                    dve.wait_ge(down_ready, e - 1)
                for f in range(FC):
                    dve.wait_ge(silu_ready, e * FC + (f + 1))
                    dve.scalar_tensor_tensor(act_sb[p][:, f, :], bank[4 + f][:, CAP:2 * CAP],
                                             wgu_sb[p][:, G_UB + f:G_UB + f + 1], silu[:, f, :],
                                             ALU.add, ALU.mult).then_inc(act_ready, 1)

            def weighted(e, p, ahead):
                dve.wait_ge(down_ready, e + 1)
                if ahead:
                    dve.wait_ge(scattered[p], loads(16 * CT, e - 2))
                    dve.wait_ge(y_done, e)
                dve.tensor_tensor(y_raw[:], bank[2][:, 0:CT * P].rearrange("p (c d) -> p c d", c=CT),
                                  db_sb[:, bass.ds(e, 1), :].broadcast_to([P, CT, P]), ALU.add
                                  ).then_inc(y_read, 1)
                dve.tensor_copy(idx_s[p][:], idx_all[:, bass.ds(e, 1), :].rearrange("p o c -> p (o c)"))
                dve.wait_ge(y_read, e + 1)
                for c in range(CT):
                    last = dve.tensor_scalar(y_sb[p][:, c, :], y_raw[:, c, :],
                                             weight[:, bass.ds(e, 1), c], None, ALU.mult)
                last.then_inc(y_done, 1)

            one_hot(0, 0, False)
            one_hot(1, 1, False)
            indices(0, 0, False)
            one_hot(2, 0, True)
            indices(1, 1, False)
            dve.wait_ge(ld_db, 16)
            dve.wait_ge(ld_wgu[0], 16)
            one_hot(3, 1, True)
            indices(2, 0, True)
            gated(0, 0, False)
            indices(3, 1, True)
            dve.wait_ge(ld_wgu[1], 16)
            one_hot(4, 0, True)
            gated(1, 1, False)
            indices(4, 0, True)
            weighted(0, 0, False)
            one_hot(5, 1, True)
            gated(2, 0, True)
            indices(5, 1, True)
            dve.wait_ge(y_done, 1)
            weighted(1, 1, False)
            with dve.Fori(0, (E - 6) // 2) as i:
                for u in range(2):
                    e = i * 2 + (3 + u)
                    p = 1 - u
                    one_hot(e + 3, 1 - p, True)
                    dve.wait_ge(ld_wgu[p], 16 * (i + 2 + u))
                    gated(e, p, True)
                    indices(e + 3, 1 - p, True)
                    weighted(e - 1, 1 - p, True)
            for e in range(E - 3, E):
                dve.wait_ge(ld_wgu[e % 2], loads(16, e))
                gated(e, e % 2, True)
                weighted(e - 1, 1 - e % 2, True)
            weighted(E - 1, 1, True)


def kernel(x, fside_Bx1x1024x16_0, cond_1024, L0_cond_W, L0_cond_fc_bias, L0_ffn_gate_w, L0_ffn_up_w, L0_ffn_up_b,
           L0_ffn_gw, L0_ffn_gb, L0_ffn_down_w, L0_ffn_down_b, L0_ffn_sh_gate_w, L0_ffn_sh_up_w, L0_ffn_sh_down_w):
    import ml_dtypes
    import numpy as np
    import concourse.bacc as bacc
    from concourse.bass_utils import run_bass_kernel_spmd

    f32 = np.float32
    p = np.arange(P)
    cf = np.zeros((P, C_N), f32)
    cf[:, C_WT:C_WT + P] = np.transpose(L0_cond_W)
    cf[:, C_COND:C_COND + B] = np.transpose(cond_1024)
    cf[:, C_FCB] = L0_cond_fc_bias
    cf[:, C_GATE + GATE_AT:C_GATE + GATE_AT + E] = np.transpose(L0_ffn_gate_w)
    cf[:, C_ID:C_ID + P] = np.eye(P)
    cf[:, C_J] = p
    cf[:, C_Q:C_Q + STEPS] = 2.0 ** (2 * (STEPS - 1 - np.arange(STEPS)))
    cb = np.zeros((P, B_N), f32)
    same = p[:, None] % E == p[None, :] % E
    cb[:, B_ONES:B_ONES + P] = same
    cb[:, B_LOW:B_LOW + P] = same & (p[:, None] // E < p[None, :] // E)
    cb[:, B_IOTA:B_IOTA + P * B] = np.repeat(p + 1, B)
    cb[:, B_BLK:B_BLK + E * B] = np.tile((P * np.arange(B)).reshape(K, HB).T.ravel(), E)
    cb = cb.astype(ml_dtypes.bfloat16)
    bits = np.zeros((P, STEPS + 1, 3), np.int32)
    for n in range(STEPS):
        bits[:, n, :] = np.array([1, 2, 3]) << (2 * (STEPS - 1 - n))

    def down_layout(w):
        h = w.shape[-1]
        v = np.swapaxes(np.asarray(w), -1, -2)
        v = v.reshape(v.shape[:-2] + (h // P, P, P))
        return np.ascontiguousarray(np.moveaxis(v, -3, -2))

    def bias_layout(v):
        return np.moveaxis(np.asarray(v).reshape(E, FC, P), 1, 2)

    arrays = {
        "xT": np.ascontiguousarray(np.transpose(x, (2, 0, 1))),
        "x": np.ascontiguousarray(np.transpose(x, (1, 0, 2))),
        "fsT": np.ascontiguousarray(np.transpose(np.asarray(fside_Bx1x1024x16_0)[:, 0], (2, 0, 1))),
        "cf": cf,
        "cb": cb,
        "bits": bits,
        "shw": np.concatenate([np.transpose(L0_ffn_sh_gate_w), np.transpose(L0_ffn_sh_up_w),
                               down_layout(L0_ffn_sh_down_w).reshape(P, SH)], axis=1),
        "wgu": np.concatenate([np.swapaxes(np.asarray(L0_ffn_gw), 1, 2), np.swapaxes(np.asarray(L0_ffn_up_w), 1, 2),
                               bias_layout(L0_ffn_gb), bias_layout(L0_ffn_up_b)], axis=2),
        "wd": down_layout(L0_ffn_down_w),
        "down_b": np.ascontiguousarray(L0_ffn_down_b),
    }
    nc = bacc.Bacc("TRN2", target_bir_lowering=False, num_devices=1)
    args = [nc.dram_tensor(f"in_{n}", a.shape, mybir.dt.from_np(a.dtype), kind="ExternalInput").ap()
            for n, a in arrays.items()]
    out = nc.dram_tensor("out_0", (B, P, P), F32, kind="ExternalOutput").ap()
    moe_program(nc, *args, out)
    r = run_bass_kernel_spmd(nc, [{f"in_{n}": a for n, a in arrays.items()}], core_ids=[0])
    return r.results[0]["out_0"]
```

```python
from contextlib import ExitStack

import concourse.bass as bass
from concourse import mybir

ALU = mybir.AluOpType
ACT = mybir.ActivationFunctionType
AX_X = mybir.AxisListType.X
F32 = mybir.dt.float32
BF16 = mybir.dt.bfloat16
I32 = mybir.dt.int32

P = 128
B = 16
T = B * P
R = 16
E = 16
CAP = T * 2 // E
CT = CAP // P
F = 512
FC = F // P
SH = 256
SC = SH // P
K = P // E
CH = T // K
HB = CH // P
ROW = P + E
UPPER = [4.0 ** (6 - n) for n in range(7)]
LOWER = [4.0 ** (7 - n) / 65536 for n in range(8)]
STEPS = len(UPPER) + len(LOWER)

C_WT, C_COND, C_FCB, C_GATE, C_ID, C_J, C_UNIT = 0, 128, 144, 145, 385, 513, 514
C_NEXT = C_UNIT + 3 * STEPS
C_N = C_NEXT + 3 * STEPS
WARM = 10
SEARCHED = 13
GATE_AT = P - E
B_ONES, B_HALF, B_LOW, B_IOTA = 0, P, 2 * P, 3 * P
B_BLK = B_IOTA + P * B
B_N = B_BLK + E * B
S_G, S_U, S_D = 0, SH, 2 * SH
S_N = 3 * SH
G_G, G_U, G_GB, G_UB = 0, F, 2 * F, 2 * F + FC
G_N = 2 * F + 2 * FC


def moe_program(nc, xT, x, fsT, cf, cb, shw, wgu, wd, down_b, out):
    ctx = ExitStack()
    with ctx:
        def sb(name, shape, dt=F32):
            return ctx.enter_context(nc.sbuf_tensor(name, shape, dt))

        def sem(name):
            return ctx.enter_context(nc.semaphore(name))

        table = nc.dram_tensor("h_and_scores", (T, ROW), F32, kind="Internal").ap()

        xT_sb = sb("xT_sb", [P, B, P])
        x_sb = sb("x_sb", [P, B, P])
        fsT_sb = sb("fsT_sb", [R, B, P])
        cf_sb = sb("cf_sb", [P, C_N])
        cb_sb = sb("cb_sb", [P, B_N], BF16)
        sh_sb = sb("sh_sb", [P, S_N])
        db_sb = sb("db_sb", [P, E, P])
        wgu_sb = [sb(f"wgu{i}", [P, G_N]) for i in range(2)]
        wd_sb = [sb(f"wd{i}", [P, FC, P]) for i in range(2)]

        biasT = sb("biasT", [P, B])
        weff = sb("weff", [P, B, P])
        hT = sb("hT", [P, T])
        hrow = sb("hrow", [P, B, ROW])
        score = sb("score", [P, CH])

        cand = sb("cand", [P, 3])
        place = sb("place", [P, 1])
        place4 = sb("place4", [P, 1])
        passed = sb("passed", [P, 3])
        fine = sb("fine", [P, CH])
        signs = sb("signs", [P, CH])
        low_half = sb("low_half", [P, CH])
        hits = sb("hits", [P, 3, CH])
        cnt = sb("cnt", [P, 3], BF16)
        warm = sb("warm", [P, 512], BF16)
        spare = sb("spare", [P, 2])
        rank_cnt = sb("rank_cnt", [P, 3], BF16)
        offs = sb("offs", [P, 2])
        above = sb("above", [P, CH])
        equal = sb("equal", [P, CH])
        zeros = sb("zeros", [P, CH])
        rank_a = sb("rank_a", [P, CH])
        rank_b = sb("rank_b", [P, CH])
        slot = sb("slot", [P, CH])
        second = sb("second", [P, E, B])
        row_of = sb("row_of", [P, E, B], BF16)
        parts = sb("parts", [P, CT, 2, E, B], BF16)

        sh_silu = sb("sh_silu", [P, SH])
        sh_up = sb("sh_up", [P, SH])
        sh_act = sb("sh_act", [P, SH])
        sh_y = sb("sh_y", [P, P])
        first = sb("first", [P, B, P])

        onehot = [sb(f"onehot{i}", [P, P, B], BF16) for i in range(2)]
        parts_of = [sb(f"parts_of{i}", [P, 2 * CT, B], BF16) for i in range(2)]
        idx_all = sb("idx_all", [P, E, CT], I32)
        idx_g = [sb(f"idx_g{i}", [P, CT], I32) for i in range(2)]
        idx_s = [sb(f"idx_s{i}", [P, CT], I32) for i in range(2)]
        rows = [sb(f"rows{i}", [P, CT, ROW]) for i in range(2)]
        weight = sb("weight", [P, E, CT])
        xinT = [sb(f"xinT{i}", [P, CAP]) for i in range(2)]
        silu = sb("silu", [P, FC, CAP])
        act_sb = [sb(f"act{i}", [P, FC, CAP]) for i in range(2)]
        y_raw = sb("y_raw", [P, CT, P])
        y_sb = [sb(f"y{i}", [P, CT, P]) for i in range(2)]

        bank = [ctx.enter_context(nc.psum_tensor(f"bank{i}", [P, 512], F32)) for i in range(8)]

        WT = cf_sb[:, C_WT:C_WT + P]
        ident = cf_sb[:, C_ID:C_ID + P]
        token = cf_sb[:, C_J:C_J + 1]
        ones = cb_sb[:, B_ONES:B_ONES + P]
        half = cb_sb[:, B_HALF:B_HALF + P]
        halves = score[:].bitcast(mybir.dt.uint16).rearrange("p (c two) -> p c two", two=2)
        lower = cb_sb[:, B_LOW:B_LOW + P]
        iota = cb_sb[:, B_IOTA:B_IOTA + P * B].rearrange("p (m b) -> p m b", b=B)
        block_at = cb_sb[:, B_BLK:B_BLK + E * B].rearrange("p (e b) -> p e b", b=B)

        ld_fs, ld_cf, ld_cb, warm_ready = sem("ld_fs"), sem("ld_cf"), sem("ld_cb"), sem("warm_ready")
        ld_x = [sem(f"ld_x{g}") for g in range(4)]
        ld_sh, ld_xrow, ld_db = sem("ld_sh"), sem("ld_xrow"), sem("ld_db")
        ld_wgu = [sem(f"ld_wgu{i}") for i in range(2)]
        ld_wd = [sem(f"ld_wd{i}") for i in range(2)]
        bias_ready, lowrank_ready, weff_ready = sem("bias_ready"), sem("lowrank_ready"), sem("weff_ready")
        y_ready, h_ready, hrow_T, hrow_ready = sem("y_ready"), sem("h_ready"), sem("hrow_T"), sem("hrow_ready")
        logits_ready, score_ready, scoreT, hscore_ready = (
            sem("logits_ready"), sem("score_ready"), sem("scoreT"), sem("hscore_ready"))
        counted, counted_act, summed, cand_ready, fine_ready, low_ready = (
            sem("counted"), sem("counted_act"), sem("summed"), sem("cand_ready"), sem("fine_ready"), sem("low_ready"))
        sh_gu, sh_silu_ready, sh_up_ready, sh_act_ready, sh_down, sh_y_ready, first_ready = (
            sem("sh_gu"), sem("sh_silu_ready"), sem("sh_up_ready"), sem("sh_act_ready"), sem("sh_down"),
            sem("sh_y_ready"), sem("first_ready"))
        rank_counted, offs_ready, slot_ready, slotT, chain = (
            sem("rank_counted"), sem("offs_ready"), sem("slot_ready"), sem("slotT"), sem("chain"))
        parts_ready, pool_turn, second_ready = sem("parts_ready"), sem("pool_turn"), sem("second_ready")
        table_done = [sem(f"table_done{i}") for i in range(2)]
        first_done = [sem(f"first_done{i}") for i in range(2)]
        onehot_ready, idx_summed, idx_ready = sem("onehot_ready"), sem("idx_summed"), sem("idx_ready")
        gathered = [sem(f"gathered{i}") for i in range(2)]
        scattered = [sem(f"scattered{i}") for i in range(2)]
        xin_T, xin_ready = sem("xin_T"), sem("xin_ready")
        gu_ready, silu_ready, act_ready = sem("gu_ready"), sem("silu_ready"), sem("act_ready")
        down_ready, y_read, y_done = sem("down_ready"), sem("y_read"), sem("y_done")

        def loads(s, e):
            return e // 2 * s + s

        UNROLL = 4
        TURNS = (E - 4) // UNROLL

        block = ctx.enter_context(nc.Block())

        @block.sync
        def _(sp):
            sp.dma_start(fsT_sb[:], fsT).then_inc(ld_fs, 16)
            sp.dma_start(cf_sb[:], cf).then_inc(ld_cf, 16)
            for g in range(4):
                sp.dma_start(xT_sb[:, 4 * g:4 * g + 4, :], xT[:, 4 * g:4 * g + 4, :]).then_inc(ld_x[g], 16)
            sp.dma_start(sh_sb[:], shw).then_inc(ld_sh, 16)
            sp.dma_start(x_sb[:], x).then_inc(ld_xrow, 16)
            for e in range(2):
                sp.dma_start(wgu_sb[e][:], wgu[e]).then_inc(ld_wgu[e], 16)
                sp.dma_start(wd_sb[e][:], wd[e]).then_inc(ld_wd[e], 16)
            sp.wait_ge(hrow_ready, 4)
            sp.wait_ge(hscore_ready, 1)
            trows = table.rearrange("(b p) c -> p b c", p=P)
            for n in range(2):
                sp.dma_start(trows[:, 8 * n:8 * n + 8, :], hrow[:, 8 * n:8 * n + 8, :]).then_inc(table_done[n], 16)
            orows = out.rearrange("b p c -> p b c")
            for n in range(2):
                sp.wait_ge(first_ready, 8 * n + 8)
                sp.dma_start(orows[:, 8 * n:8 * n + 8, :], first[:, 8 * n:8 * n + 8, :]).then_inc(first_done[n], 16)

            def load_gu(e, p):
                sp.wait_ge(act_ready, e * FC - FC)
                sp.dma_start(wgu_sb[p][:], wgu[bass.ds(e, 1)].rearrange("o p c -> (o p) c")).then_inc(ld_wgu[p], 16)

            def load_d(e, p):
                sp.wait_ge(down_ready, e - 1)
                sp.dma_start(wd_sb[p][:], wd[bass.ds(e, 1)].rearrange("o p c d -> (o p) c d")).then_inc(ld_wd[p], 16)

            with sp.Fori(0, (E - 2) // 2) as i:
                for u in range(2):
                    load_gu(i * 2 + (2 + u), u)
                    load_d(i * 2 + (2 + u), u)
            for s in scattered:
                sp.wait_ge(s, 16 * CT * E // 2)

        @block.tensor
        def _(pe):
            pe.wait_ge(warm_ready, 1)
            for _ in range(WARM):
                pe.matmul(bank[7][:, :], warm[:, 0:P], warm[:], start=True, stop=True)

            def low_rank(g):
                for n in range(4):
                    f = fsT_sb[:, 4 * g + n, :]
                    mm = pe.matmul(bank[g][:, n * P:(n + 1) * P], f, f, start=True, stop=True)
                mm.then_inc(lowrank_ready, 1)

            def project(g):
                pe.wait_ge(weff_ready, g + 1)
                pe.wait_ge(ld_x[g], 16)
                for n in range(4):
                    mm = pe.matmul(bank[4 + g][:, n * P:(n + 1) * P], weff[:, 4 * g + n, :],
                                   xT_sb[:, 4 * g + n, :], start=True, stop=True)
                mm.then_inc(y_ready, 1)

            def logits(g):
                for k in range(g * 4 // HB, (g + 1) * 4 // HB):
                    pe.wait_ge(h_ready, max(HB * (k + 1), 4))
                    at = C_GATE + GATE_AT - E * k
                    mm = pe.matmul(bank[4][:, 0:CH], cf_sb[:, at:at + P], hT[:, k * CH:(k + 1) * CH],
                                   start=(k == 0), stop=(k == K - 1))
                if g == 3:
                    mm.then_inc(logits_ready, 1)

            def h_rows(g):
                for b in range(4 * g, 4 * g + 4):
                    tr = pe.transpose(bank[g][:, b % 4 * P:(b % 4 + 1) * P], hT[:, b * P:(b + 1) * P], ident)
                tr.then_inc(hrow_T, 1)

            pe.wait_ge(ld_fs, 16)
            low_rank(0)
            low_rank(1)
            project(0)
            low_rank(2)
            project(1)
            low_rank(3)
            project(2)
            pe.wait_ge(ld_cf, 16)
            logits(0)
            project(3)
            h_rows(0)
            for g in range(1, 4):
                logits(g)
                h_rows(g)

            def shared_in(t):
                if t:
                    pe.wait_ge(sh_up_ready, t)
                for c in range(2 * SC):
                    mm = pe.matmul(bank[1][:, c * P:(c + 1) * P], sh_sb[:, c * P:(c + 1) * P],
                                   hT[:, t * P:(t + 1) * P], start=True, stop=True)
                mm.then_inc(sh_gu, 1)

            def shared_out(t):
                pe.wait_ge(sh_act_ready, t + 1)
                if t:
                    pe.wait_ge(sh_y_ready, t)
                for c in range(SC):
                    mm = pe.matmul(bank[2][:, 0:P], sh_act[:, c * P:(c + 1) * P],
                                   sh_sb[:, S_D + c * P:S_D + (c + 1) * P], start=(c == 0), stop=(c == SC - 1))
                mm.then_inc(sh_down, 1)

            def sum_counts(n):
                pe.wait_ge(counted, n + 1)
                pe.matmul(bank[0][:, 0:2], ones, cnt[:, 0:2], start=True, stop=True)
                pe.wait_ge(counted_act, n + 1)
                pe.matmul(bank[0][:, 2:3], half, cnt[:, 2:3], start=True, stop=True).then_inc(summed, 1)

            pe.wait_ge(ld_cb, 16)
            pe.wait_ge(ld_sh, 16)
            pe.wait_ge(hrow_ready, 3)
            pe.wait_ge(score_ready, 1)
            for h in range(HB):
                tr = pe.transpose(bank[5][:, h * P:(h + 1) * P], score[:, h * P:(h + 1) * P], ident)
            tr.then_inc(scoreT, 1)
            for n in range(STEPS):
                sum_counts(n)
                if n < SEARCHED:
                    shared_in(n)
                    if n:
                        shared_out(n - 1)
            shared_in(SEARCHED)
            shared_out(SEARCHED - 1)
            pe.wait_ge(rank_counted, 1)
            pe.matmul(bank[0][:, 8:10], lower, rank_cnt[:, 1:3], start=True, stop=False)
            pe.matmul(bank[0][:, 8:10], ones, rank_cnt[:, 0:2], start=False, stop=True).then_inc(offs_ready, 1)
            shared_in(SEARCHED + 1)
            shared_out(SEARCHED)
            pe.wait_ge(slot_ready, 1)
            for h in range(HB):
                tr = pe.transpose(bank[3][:, h * P:(h + 1) * P], slot[:, h * P:(h + 1) * P], ident)
            tr.then_inc(slotT, 1)
            for t in range(SEARCHED + 2, B):
                shared_in(t)
                shared_out(t - 1)
            shared_out(B - 1)

            def sum_indices(e, p, ahead):
                pe.wait_ge(onehot_ready, e + 1)
                if ahead:
                    pe.wait_ge(idx_ready, e)
                for b in range(B):
                    mm = pe.matmul(bank[0][:, 0:2 * CT], onehot[p][:, :, b], parts_of[p][:, :, b],
                                   start=(b == 0), stop=(b == B - 1))
                mm.then_inc(idx_summed, 1)

            def transpose_rows(e, p, ahead):
                pe.wait_ge(gathered[p], loads(16 * CT, e))
                if ahead:
                    pe.wait_ge(xin_ready, e)
                for c in range(CT):
                    tr = pe.transpose(bank[3][:, c * P:(c + 1) * P], rows[p][:, c, 0:P], ident)
                tr.then_inc(xin_T, 1)

            def gate_up(e, p, ahead):
                pe.wait_ge(xin_ready, e + 1)
                pe.wait_ge(ld_wgu[p], loads(16, e))
                for f in range(FC):
                    if ahead:
                        pe.wait_ge(act_ready, e * FC + (f + 1 - FC))
                    pe.matmul(bank[4 + f][:, 0:CAP], wgu_sb[p][:, G_G + f * P:G_G + (f + 1) * P], xinT[p][:],
                              start=True, stop=True)
                    pe.matmul(bank[4 + f][:, CAP:2 * CAP], wgu_sb[p][:, G_U + f * P:G_U + (f + 1) * P],
                              xinT[p][:], start=True, stop=True).then_inc(gu_ready, 1)

            def down(e, p, ahead):
                pe.wait_ge(act_ready, e * FC + FC)
                pe.wait_ge(ld_wd[p], loads(16, e))
                if ahead:
                    pe.wait_ge(y_read, e)
                for c in range(CT):
                    for f in range(FC):
                        mm = pe.matmul(bank[2][:, c * P:(c + 1) * P], act_sb[p][:, f, c * P:(c + 1) * P],
                                       wd_sb[p][:, f, :], start=(f == 0), stop=(f == FC - 1))
                mm.then_inc(down_ready, 1)

            def expert(e, p):
                transpose_rows(e + 1, 1 - p, True)
                gate_up(e, p, True)
                sum_indices(e + 3, 1 - p, True)
                down(e - 1, 1 - p, True)

            pe.wait_ge(parts_ready, 3)
            for e in range(3):
                sum_indices(e, e % 2, e > 0)
            transpose_rows(0, 0, False)
            transpose_rows(1, 1, True)
            gate_up(0, 0, False)
            sum_indices(3, 1, True)
            pe.wait_ge(sh_y_ready, B)
            with pe.Fori(0, TURNS) as i:
                for u in range(UNROLL):
                    expert(i * UNROLL + (1 + u), (1 + u) % 2)
            for e in range(E - 3, E):
                if e + 1 < E:
                    transpose_rows(e + 1, 1 - e % 2, True)
                gate_up(e, e % 2, True)
                down(e - 1, 1 - e % 2, True)
            down(E - 1, 1, True)

        @block.scalar
        def _(act):
            act.dma_start(cb_sb[:], cb).then_inc(ld_cb, 16)
            act.dma_start(db_sb[:], down_b.partition_broadcast(P)).then_inc(ld_db, 16)
            act.wait_ge(warm_ready, 1)
            act.activation(spare[:, 0:1], warm[:, 0:1], ACT.Gelu)
            act.wait_ge(bias_ready, 1)
            for b in range(B):
                if b % 4 == 0:
                    act.wait_ge(y_ready, b // 4 + 1)
                act.activation(hT[:, b * P:(b + 1) * P], bank[4 + b // 4][:, b % 4 * P:(b % 4 + 1) * P],
                               ACT.Gelu, bias=biasT[:, b:b + 1]).then_inc(h_ready, 1)
            act.wait_ge(logits_ready, 1)
            act.activation(score[:], bank[4][:, 0:CH], ACT.Sigmoid).then_inc(score_ready, 1)
            act.wait_ge(score_ready, 1)

            def second_part():
                act.wait_ge(second_ready, 1)
                act.activation(parts[:, 1, 0], second[:], ACT.Copy, scale=token).then_inc(parts_ready, 1)

            def count_third(n):
                act.wait_ge(cand_ready, n + 1)
                if n:
                    act.wait_ge(summed, n)
                if n == len(UPPER):
                    act.wait_ge(fine_ready, 1)
                with nc.allow_low_precision(reason="integers up to 256"):
                    act.activation(signs[:], halves[:, :, 1] if n < len(UPPER) else fine[:], ACT.Sign,
                                   bias=cand[:, 2:3], accum_out=cnt[:, 2:3]).then_inc(counted_act, 1)

            def shared_read(t):
                act.wait_ge(sh_gu, t + 1)
                if t:
                    act.wait_ge(sh_act_ready, t)
                act.activation(sh_silu[:], bank[1][:, 0:SH], ACT.Silu).then_inc(sh_silu_ready, 1)
                act.activation(sh_up[:], bank[1][:, SH:2 * SH], ACT.Copy).then_inc(sh_up_ready, 1)

            def shared_y(t):
                act.wait_ge(sh_down, t + 1)
                if t:
                    act.wait_ge(first_ready, t)
                act.activation(sh_y[:], bank[2][:, 0:P], ACT.Copy).then_inc(sh_y_ready, 1)

            count_third(0)
            act.activation(spare[:, 1:2], warm[:, 0:1], ACT.Silu)
            act.activation(low_half[:], halves[:, :, 0], ACT.Copy, scale=1.0 / 65536).then_inc(low_ready, 1)
            for n in range(1, STEPS):
                count_third(n)
                t = n - 1
                if t < SEARCHED:
                    shared_read(t)
                    if t:
                        shared_y(t - 1)
                if n == 1:
                    act.wait_ge(scoreT, 1)
                    act.activation(hrow[:, :, P:ROW].rearrange("p (k h) e -> p h k e", h=HB),
                                   bank[5][:, 0:CH].rearrange("p (h k e) -> p h k e", h=HB, k=K), ACT.Copy
                                   ).then_inc(hscore_ready, 1)
            for t in range(SEARCHED, B):
                shared_read(t)
                shared_y(t - 1)
                if t == SEARCHED + 1:
                    second_part()
            shared_y(B - 1)

            def read_rows(e, p, ahead):
                act.wait_ge(gathered[p], loads(16 * CT, e))
                act.activation(weight[:, bass.ds(e, 1), :].rearrange("p o c -> p (o c)"),
                               rows[p][:, :, bass.ds(P + e, 1)].rearrange("p c o -> p (c o)"), ACT.Copy)
                act.wait_ge(xin_T, e + 1)
                if ahead:
                    act.wait_ge(gu_ready, e * FC - FC)
                act.activation(xinT[p][:], bank[3][:, 0:CAP], ACT.Copy).then_inc(xin_ready, 1)

            def silus(e, p, ahead):
                for f in range(FC):
                    act.wait_ge(gu_ready, e * FC + (f + 1))
                    if ahead:
                        act.wait_ge(act_ready, e * FC + (f + 1 - FC))
                    act.activation(silu[:, f, :], bank[4 + f][:, 0:CAP], ACT.Silu,
                                   bias=wgu_sb[p][:, G_GB + f:G_GB + f + 1]).then_inc(silu_ready, 1)

            act.wait_ge(ld_wgu[0], 16)
            read_rows(0, 0, False)
            read_rows(1, 1, False)
            silus(0, 0, False)
            with act.Fori(0, TURNS) as i:
                for u in range(UNROLL):
                    e = i * UNROLL + (1 + u)
                    read_rows(e + 1, u % 2, True)
                    act.wait_ge(ld_wgu[1 - u % 2], loads(16, e))
                    silus(e, 1 - u % 2, True)
            for e in range(E - 3, E):
                if e + 1 < E:
                    read_rows(e + 1, (e + 1) % 2, True)
                act.wait_ge(ld_wgu[e % 2], loads(16, e))
                silus(e, e % 2, True)

        @block.gpsimd
        def _(pool):
            pool.wait_ge(ld_xrow, 16)

            def shared_mul(t, ahead):
                pool.wait_ge(sh_up_ready, t + 1)
                if ahead:
                    pool.wait_ge(sh_down, t)
                pool.tensor_tensor(sh_act[:], sh_silu[:], sh_up[:], ALU.mult).then_inc(sh_act_ready, 1)

            def add_x(t):
                pool.wait_ge(sh_y_ready, t + 1)
                pool.tensor_tensor(first[:, bass.ds(t, 1), :].rearrange("p o c -> p (o c)"), sh_y[:],
                                   x_sb[:, bass.ds(t, 1), :].rearrange("p o c -> p (o c)"), ALU.add
                                   ).then_inc(first_ready, 1)

            shared_mul(0, False)
            with pool.Fori(1, SEARCHED + 2) as i:
                shared_mul(i, True)
                add_x(i - 1)
            pool.wait_ge(second_ready, 1)
            pool.wait_ge(ld_cb, 16)
            pool.tensor_tensor(parts[:, 1, 1], second[:], block_at, ALU.mult).then_inc(parts_ready, 1)
            with pool.Fori(SEARCHED + 2, B) as i:
                shared_mul(i, True)
                add_x(i - 1)
            add_x(B - 1)

            def gather(e, p, ahead):
                pool.wait_ge(idx_ready, e + 1)
                if ahead:
                    pool.wait_ge(xin_ready, e - 1)
                pool.sem_inc(pool_turn, 1)
                for c in range(CT):
                    pool.indirect_dma_start(rows[p][:, c, :], None, table,
                                            bass.IndirectOffsetOnAxis(ap=idx_g[p][:, c:c + 1], axis=0)
                                            ).then_inc(gathered[p], 16)

            def scatter(e, p):
                pool.wait_ge(y_done, e + 1)
                pool.wait_ge(scattered[1 - p], (e + 1) // 2 * (16 * CT))
                pool.sem_inc(pool_turn, 1)
                for c in range(CT):
                    pool.indirect_dma_start(out.rearrange("b p c -> (b p) c"),
                                            bass.IndirectOffsetOnAxis(ap=idx_s[p][:, c:c + 1], axis=0),
                                            y_sb[p][:, c, :], None, compute_op=ALU.add
                                            ).then_inc(scattered[p], 16)

            for n in range(2):
                pool.wait_ge(table_done[n], 16)
            gather(0, 0, False)
            gather(1, 1, False)
            gather(2, 0, True)
            gather(3, 1, True)
            for n in range(2):
                pool.wait_ge(first_done[n], 16)
            with pool.Fori(0, TURNS) as i:
                for u in range(UNROLL):
                    gather(i * UNROLL + (4 + u), u % 2, True)
                    scatter(i * UNROLL + u, u % 2)
            for e in range(E - 4, E):
                scatter(e, e % 2)

        @block.vector
        def _(dve):
            linked = [0]

            def link(ins):
                linked[0] += 1
                ins.then_inc(chain, 1)
                dve.wait_ge(chain, linked[0])

            dve.memset(warm[:], 0.0).then_inc(warm_ready, 1)
            dve.memset(zeros[:], 0.0)
            dve.memset(rank_cnt[:], 0.0)
            dve.wait_ge(ld_cf, 16)
            dve.tensor_scalar(biasT[:], cf_sb[:, C_COND:C_COND + B], cf_sb[:, C_FCB:C_FCB + 1], None, ALU.add
                              ).then_inc(bias_ready, 1)
            for g in range(4):
                dve.wait_ge(lowrank_ready, g + 1)
                dve.scalar_tensor_tensor(weff[:, 4 * g:4 * g + 4, :],
                                         bank[g][:, :].rearrange("p (b o) -> p b o", b=4), 1.0 / (P * R),
                                         WT[:, None, :].broadcast_to([P, 4, P]), ALU.mult, ALU.add
                                         ).then_inc(weff_ready, 1)
            for g in range(4):
                dve.wait_ge(hrow_T, g + 1)
                dve.tensor_copy(hrow[:, 4 * g:4 * g + 4, 0:P], bank[g][:, :].rearrange("p (b o) -> p b o", b=4)
                                ).then_inc(hrow_ready, 1)
            link(dve.tensor_copy(cand[:], cf_sb[:, C_NEXT:C_NEXT + 3]))
            dve.engine_nop().then_inc(cand_ready, 1)
            dve.wait_ge(ld_cb, 16)
            dve.wait_ge(score_ready, 1)
            for n in range(STEPS):
                upper = n < len(UPPER)
                data = halves[:, :, 1] if upper else fine[:]
                first_step = n in (0, len(UPPER))
                last_step = n in (len(UPPER) - 1, STEPS - 1)
                for j in range(2):
                    c = dve.tensor_scalar(hits[:, j, :], data, cand[:, j:j + 1], -CH / 2, ALU.is_ge, ALU.add,
                                          accum_out=cnt[:, j:j + 1])
                c.then_inc(counted, 1)
                if not first_step:
                    link(dve.tensor_scalar(place4[:], place[:], 4.0, None, ALU.mult))
                dve.wait_ge(summed, n + 1)
                link(dve.tensor_scalar(passed[:], bank[0][:, 0:3], float(CAP - T // 2),
                                       0.0 if first_step else place4[:], ALU.is_ge, ALU.add,
                                       accum_out=place[:]))
                if not last_step:
                    unit = C_UNIT + 3 * n
                    nxt = C_NEXT + 3 * (n + 1)
                    dve.scalar_tensor_tensor(cand[:], cf_sb[:, unit:unit + 3], place[:],
                                             cf_sb[:, nxt:nxt + 3], ALU.mult, ALU.add).then_inc(cand_ready, 1)
                    dve.wait_ge(cand_ready, n + 2)
                elif upper:
                    dve.wait_ge(low_ready, 1)
                    dve.scalar_tensor_tensor(fine[:], halves[:, :, 1], place[:], low_half[:], ALU.subtract,
                                             ALU.add).then_inc(fine_ready, 1)
                    nxt = C_NEXT + 3 * (n + 1)
                    dve.tensor_copy(cand[:], cf_sb[:, nxt:nxt + 3]).then_inc(cand_ready, 1)
                    dve.wait_ge(cand_ready, n + 2)
            link(dve.tensor_scalar(place4[:], place[:], LOWER[-1], None, ALU.mult))
            dve.tensor_scalar(above[:], fine[:], place4[:], None, ALU.is_gt)
            link(dve.tensor_scalar(equal[:], fine[:], place4[:], None, ALU.is_equal))
            dve.tensor_tensor_scan(rank_a[:], above[:], zeros[:], 0.0, ALU.add, ALU.add)
            link(dve.tensor_tensor_scan(rank_b[:], equal[:], zeros[:], 0.0, ALU.add, ALU.add))
            dve.tensor_copy(rank_cnt[:, 1:2], rank_a[:, CH - 1:CH])
            dve.tensor_copy(rank_cnt[:, 2:3], rank_b[:, CH - 1:CH]).then_inc(rank_counted, 1)
            dve.wait_ge(offs_ready, 1)
            link(dve.tensor_copy(offs[:], bank[0][:, 8:10]))
            dve.scalar_tensor_tensor(above[:], rank_a[:], offs[:, 0:1], above[:], ALU.add, ALU.mult)
            link(dve.scalar_tensor_tensor(equal[:], rank_b[:], offs[:, 1:2], equal[:], ALU.add, ALU.mult))
            dve.tensor_tensor(slot[:], above[:], equal[:], ALU.add).then_inc(slot_ready, 1)
            dve.wait_ge(slotT, 1)
            at = bank[3][:, 0:CH].rearrange("p (b e) -> p e b", e=E)

            link(dve.tensor_scalar(second[:], at, float(P), None, ALU.is_gt))
            dve.engine_nop().then_inc(second_ready, 1)
            dve.scalar_tensor_tensor(row_of[:], second[:], -float(P), at, ALU.mult, ALU.add)
            dve.tensor_scalar(parts[:, 0, 0], at, float(P), token, ALU.is_le, ALU.mult)
            link(dve.scalar_tensor_tensor(parts[:, 0, 1], at, float(P), block_at, ALU.is_le, ALU.mult))
            dve.engine_nop().then_inc(parts_ready, 1)

            def one_hot(e, p, ahead):
                if ahead:
                    dve.wait_ge(idx_summed, e - 1)
                dve.tensor_copy(parts_of[p][:], parts[:, :, :, bass.ds(e, 1), :].rearrange("p n q o b -> p (n q o) b"))
                dve.tensor_tensor(onehot[p][:], iota, row_of[:, bass.ds(e, 1), :].broadcast_to([P, P, B]),
                                  ALU.is_equal).then_inc(onehot_ready, 1)

            def indices(e, p, ahead):
                dve.wait_ge(idx_summed, e + 1)
                if ahead:
                    dve.wait_ge(gathered[p], loads(16 * CT, e - 2))
                pair = bank[0][:, 0:2 * CT].rearrange("p (n q) -> p n q", q=2)
                with nc.allow_low_precision(reason="token numbers"):
                    dve.tensor_reduce(idx_all[:, bass.ds(e, 1), :].rearrange("p o c -> p (o c)"), pair, AX_X,
                                      ALU.add)
                    dve.tensor_reduce(idx_g[p][:], pair, AX_X, ALU.add).then_inc(idx_ready, 1)

            def gated(e, p, ahead):
                if ahead:
                    dve.wait_ge(down_ready, e - 1)
                for f in range(FC):
                    dve.wait_ge(silu_ready, e * FC + (f + 1))
                    dve.scalar_tensor_tensor(act_sb[p][:, f, :], bank[4 + f][:, CAP:2 * CAP],
                                             wgu_sb[p][:, G_UB + f:G_UB + f + 1], silu[:, f, :],
                                             ALU.add, ALU.mult).then_inc(act_ready, 1)

            def weighted(e, p):
                dve.wait_ge(down_ready, e + 1)
                dve.wait_ge(y_done, e)
                dve.tensor_tensor(y_raw[:], bank[2][:, 0:CT * P].rearrange("p (c d) -> p c d", c=CT),
                                  db_sb[:, bass.ds(e, 1), :].broadcast_to([P, CT, P]), ALU.add
                                  ).then_inc(y_read, 1)
                dve.wait_ge(scattered[p], e // 2 * (16 * CT))
                dve.tensor_copy(idx_s[p][:], idx_all[:, bass.ds(e, 1), :].rearrange("p o c -> p (o c)"))
                dve.wait_ge(y_read, e + 1)
                for c in range(CT):
                    last = dve.tensor_scalar(y_sb[p][:, c, :], y_raw[:, c, :],
                                             weight[:, bass.ds(e, 1), c], None, ALU.mult)
                last.then_inc(y_done, 1)

            dve.wait_ge(parts_ready, 3)
            one_hot(0, 0, False)
            one_hot(1, 1, False)
            indices(0, 0, False)
            one_hot(2, 0, True)
            indices(1, 1, False)
            dve.wait_ge(ld_db, 16)
            dve.wait_ge(ld_wgu[0], 16)
            one_hot(3, 1, True)
            indices(2, 0, True)
            gated(0, 0, False)
            indices(3, 1, True)
            with dve.Fori(0, TURNS) as i:
                for u in range(UNROLL):
                    e = i * UNROLL + (1 + u)
                    p = (1 + u) % 2
                    one_hot(e + 3, 1 - p, True)
                    dve.wait_ge(ld_wgu[p], loads(16, e))
                    gated(e, p, True)
                    indices(e + 3, 1 - p, True)
                    weighted(e - 1, 1 - p)
            for e in range(E - 3, E):
                dve.wait_ge(ld_wgu[e % 2], loads(16, e))
                gated(e, e % 2, True)
                weighted(e - 1, 1 - e % 2)
            weighted(E - 1, 1)


def kernel(x, fside_Bx1x1024x16_0, cond_1024, L0_cond_W, L0_cond_fc_bias, L0_ffn_gate_w, L0_ffn_up_w, L0_ffn_up_b,
           L0_ffn_gw, L0_ffn_gb, L0_ffn_down_w, L0_ffn_down_b, L0_ffn_sh_gate_w, L0_ffn_sh_up_w, L0_ffn_sh_down_w):
    import ml_dtypes
    import numpy as np
    import concourse.bacc as bacc
    from concourse.bass_utils import run_bass_kernel_spmd

    f32 = np.float32
    p = np.arange(P)
    cf = np.zeros((P, C_N), f32)
    cf[:, C_WT:C_WT + P] = np.transpose(L0_cond_W)
    cf[:, C_COND:C_COND + B] = np.transpose(cond_1024)
    cf[:, C_FCB] = L0_cond_fc_bias
    cf[:, C_GATE + GATE_AT:C_GATE + GATE_AT + E] = np.transpose(L0_ffn_gate_w)
    cf[:, C_ID:C_ID + P] = np.eye(P)
    cf[:, C_J] = p
    for n in range(STEPS):
        unit = (UPPER + LOWER)[n]
        half = 0.5 if n < len(UPPER) else 0.5 / 65536
        cf[:, C_UNIT + 3 * n:C_UNIT + 3 * n + 3] = unit, unit, -unit
        cf[:, C_NEXT + 3 * n:C_NEXT + 3 * n + 3] = unit, 2 * unit, half - 3 * unit
    cb = np.zeros((P, B_N), f32)
    same = p[:, None] % E == p[None, :] % E
    cb[:, B_ONES:B_ONES + P] = same
    cb[:, B_HALF:B_HALF + P] = 0.5 * same
    cb[:, B_LOW:B_LOW + P] = same & (p[:, None] // E < p[None, :] // E)
    cb[:, B_IOTA:B_IOTA + P * B] = np.repeat(p + 1, B)
    cb[:, B_BLK:B_BLK + E * B] = np.tile((P * np.arange(B)).reshape(K, HB).T.ravel(), E)
    cb = cb.astype(ml_dtypes.bfloat16)
    def down_layout(w):
        h = w.shape[-1]
        v = np.swapaxes(np.asarray(w), -1, -2)
        v = v.reshape(v.shape[:-2] + (h // P, P, P))
        return np.ascontiguousarray(np.moveaxis(v, -3, -2))

    def bias_layout(v):
        return np.moveaxis(np.asarray(v).reshape(E, FC, P), 1, 2)

    arrays = {
        "xT": np.ascontiguousarray(np.transpose(x, (2, 0, 1))),
        "x": np.ascontiguousarray(np.transpose(x, (1, 0, 2))),
        "fsT": np.ascontiguousarray(np.transpose(np.asarray(fside_Bx1x1024x16_0)[:, 0], (2, 0, 1))),
        "cf": cf,
        "cb": cb,
        "shw": np.concatenate([np.transpose(L0_ffn_sh_gate_w), np.transpose(L0_ffn_sh_up_w),
                               down_layout(L0_ffn_sh_down_w).reshape(P, SH)], axis=1),
        "wgu": np.concatenate([np.swapaxes(np.asarray(L0_ffn_gw), 1, 2), np.swapaxes(np.asarray(L0_ffn_up_w), 1, 2),
                               bias_layout(L0_ffn_gb), bias_layout(L0_ffn_up_b)], axis=2),
        "wd": down_layout(L0_ffn_down_w),
        "down_b": np.ascontiguousarray(L0_ffn_down_b),
    }
    nc = bacc.Bacc("TRN2", target_bir_lowering=False, num_devices=1)
    args = [nc.dram_tensor(f"in_{n}", a.shape, mybir.dt.from_np(a.dtype), kind="ExternalInput").ap()
            for n, a in arrays.items()]
    out = nc.dram_tensor("out_0", (B, P, P), F32, kind="ExternalOutput").ap()
    moe_program(nc, *args, out)
    r = run_bass_kernel_spmd(nc, [{f"in_{n}": a for n, a in arrays.items()}], core_ids=[0])
    return r.results[0]["out_0"]
```

```python
from contextlib import ExitStack

import concourse.bass as bass
from concourse import mybir

ALU = mybir.AluOpType
ACT = mybir.ActivationFunctionType
AX_X = mybir.AxisListType.X
F32 = mybir.dt.float32
BF16 = mybir.dt.bfloat16
I32 = mybir.dt.int32
F32R = mybir.dt.float32r

P = 128
B = 16
T = B * P
R = 16
E = 16
CAP = T * 2 // E
CT = CAP // P
F = 512
FC = F // P
SH = 256
SC = SH // P
K = P // E
CH = T // K
HB = CH // P
ROW = P + E
UPPER = [4.0 ** (6 - n) for n in range(7)]
LOWER = [4.0 ** (7 - n) for n in range(8)]
STEPS = len(UPPER) + len(LOWER)

C_WT, C_COND, C_FCB = 0, 128, 144
C_FIRST = C_FCB + 1
C_GATE, C_ID, C_J, C_UNIT = C_FIRST, C_FIRST + 240, C_FIRST + 368, C_FIRST + 370
C_NEXT = C_UNIT + 3 * STEPS
C_N = C_NEXT + 3 * STEPS
WARM = 8
IN_STEPS = [0, 1, 2, 3, 4, 6, 7, 8, 9, 10, 11, 12, 13]
OUT_STEPS = [2, 3, 4, 5, 7, 8, 9, 10, 11, 12, 13, 14]
ROWS_STEPS = [0, 1, 2, 9, 10, 11]
ROWS_ORDER = [2, 1, 3]
UPPER_STEP, LOWER_STEPS = 6, [3, 4, 12, 13]
SLOTS = B - len(OUT_STEPS)
GATE_AT = P - E
B_ONES, B_HALF, B_LOW, B_IOTA = 0, P, 2 * P, 3 * P
B_BLK = B_IOTA + P * B
B_NEG = B_BLK + E * B
B_N = B_NEG + E * B
S_G, S_U, S_D = 0, SH, 2 * SH
S_N = 3 * SH
G_G, G_U, G_GB, G_UB = 0, F, 2 * F, 2 * F + FC
G_N = 2 * F + 2 * FC


def moe_program(nc, xT, fsT, cf, cb, shw, wgu, wd, down_b, out):
    ctx = ExitStack()
    with ctx:
        def sb(name, shape, dt=F32):
            return ctx.enter_context(nc.sbuf_tensor(name, shape, dt))

        def sem(name):
            return ctx.enter_context(nc.semaphore(name))

        table = nc.dram_tensor("h_and_scores", (T, ROW), F32, kind="Internal").ap()

        xT_sb = sb("xT_sb", [P, B, P])
        fsT_sb = sb("fsT_sb", [R, B, P])
        cf_sb = sb("cf_sb", [P, C_N])
        cb_sb = sb("cb_sb", [P, B_N], BF16)
        sh_sb = sb("sh_sb", [P, S_N])
        db_sb = sb("db_sb", [P, E, P])
        wgu_sb = [sb(f"wgu{i}", [P, G_N]) for i in range(4)]
        wd_sb = [sb(f"wd{i}", [P, FC, P]) for i in range(2)]

        biasT = sb("biasT", [P, B])
        weff = sb("weff", [P, B, P])
        hT = sb("hT", [P, T])
        hrow = sb("hrow", [P, B, ROW])
        score = sb("score", [P, CH])

        cand = sb("cand", [P, 3])
        place = sb("place", [P, 1])
        coarse_at = sb("coarse_at", [P, 1])
        place4 = sb("place4", [P, 1])
        passed = sb("passed", [P, 3])
        coarse = sb("coarse", [P, CH], mybir.dt.uint16)
        fine = sb("fine", [P, CH], mybir.dt.uint16)
        higher = sb("higher", [P, CH], BF16)
        same = sb("same", [P, CH], BF16)
        signs = sb("signs", [P, CH])
        hits = sb("hits", [P, 2, CH], BF16)
        cnt = sb("cnt", [P, 4], BF16)
        warm = sb("warm", [P, P], BF16)
        spare = sb("spare", [P, 2])
        rank_cnt = sb("rank_cnt", [P, 3], BF16)
        above = sb("above", [P, CH])
        equal = sb("equal", [P, CH])
        zeros = sb("zeros", [P, CH])
        ranks = sb("ranks", [P, 2, CH])
        slot = sb("slot", [P, CH])
        second = sb("second", [P, E, B])
        row_of = sb("row_of", [P, E, B], BF16)
        parts = sb("parts", [P, CT, 4, E, B], BF16)

        sh_silu = [sb(f"sh_silu{i}", [P, SH]) for i in range(2)]
        sh_up = [sb(f"sh_up{i}", [P, SH]) for i in range(2)]
        sh_act = [sb(f"sh_act{i}", [P, SH]) for i in range(2)]
        first = sb("first", [P, B, P])

        onehot = [sb(f"onehot{i}", [P, P, B], BF16) for i in range(2)]
        parts_of = [sb(f"parts_of{i}", [P, CT * 4, B], BF16) for i in range(2)]
        idx_g = [sb(f"idx_g{i}", [P, CT], I32) for i in range(4)]
        idx_s = [sb(f"idx_s{i}", [P, CT], I32) for i in range(2)]
        rows = [sb(f"rows{i}", [P, CT, ROW]) for i in range(4)]
        weight = [sb(f"weight{i}", [P, CT]) for i in range(4)]
        x_hi = [sb(f"x_hi{i}", [P, CAP], F32R) for i in range(2)]
        x_lo = [sb(f"x_lo{i}", [P, CAP], F32R) for i in range(2)]
        w_hi = [sb(f"w_hi{i}", [P, 2 * F], F32R) for i in range(2)]
        w_lo = [sb(f"w_lo{i}", [P, 2 * F], F32R) for i in range(2)]
        silu = sb("silu", [P, FC, CAP])
        act_sb = [sb(f"act{i}", [P, FC, CAP]) for i in range(2)]
        y_raw = sb("y_raw", [P, CT, P])
        y_sb = [sb(f"y{i}", [P, CT, P]) for i in range(2)]

        down_banks = ctx.enter_context(nc.psum_tensor("down_banks", [P, CT, 512], F32))
        bank = [None if i in (1, 2) else ctx.enter_context(nc.psum_tensor(f"bank{i}", [P, 512], F32))
                for i in range(8)]
        bank[1:3] = down_banks[:, 0, :], down_banks[:, 1, :]

        WT = cf_sb[:, C_WT:C_WT + P]
        ident = cf_sb[:, C_ID:C_ID + P]
        token, token_neg = cf_sb[:, C_J:C_J + 1], cf_sb[:, C_J + 1:C_J + 2]
        ones = cb_sb[:, B_ONES:B_ONES + P]
        half = cb_sb[:, B_HALF:B_HALF + P]
        halves = score[:].bitcast(mybir.dt.uint16).rearrange("p (c two) -> p c two", two=2)
        lower = cb_sb[:, B_LOW:B_LOW + P]
        iota = cb_sb[:, B_IOTA:B_IOTA + P * B].rearrange("p (m b) -> p m b", b=B)
        block_neg = cb_sb[:, B_NEG:B_NEG + E * B].rearrange("p (e b) -> p e b", e=E)
        block_at = cb_sb[:, B_BLK:B_BLK + E * B].rearrange("p (e b) -> p e b", b=B)

        ld_fs, ld_wt, ld_cf, ld_cb, warm_ready = (
            sem("ld_fs"), sem("ld_wt"), sem("ld_cf"), sem("ld_cb"), sem("warm_ready"))
        ld_x = [sem(f"ld_x{g}") for g in range(4)]
        ld_sh, ld_db = sem("ld_sh"), sem("ld_db")
        ld_wgu = [sem(f"ld_wgu{i}") for i in range(4)]
        ld_wd = [sem(f"ld_wd{i}") for i in range(2)]
        bias_ready, lowrank_ready, weff_ready = sem("bias_ready"), sem("lowrank_ready"), sem("weff_ready")
        y_ready, h_ready, hrow_T, hrow_ready = sem("y_ready"), sem("h_ready"), sem("hrow_T"), sem("hrow_ready")
        logits_ready, score_ready, scoreT, hscore_ready = (
            sem("logits_ready"), sem("score_ready"), sem("scoreT"), sem("hscore_ready"))
        counted, counted_act, summed, cand_ready, fine_ready, coarse_ready, higher_ready = (
            sem("counted"), sem("counted_act"), sem("summed"), sem("cand_ready"), sem("fine_ready"),
            sem("coarse_ready"), sem("higher_ready"))
        sh_gu, sh_up_ready, sh_act_ready, sh_down, first_ready = (
            sem("sh_gu"), sem("sh_up_ready"), sem("sh_act_ready"), sem("sh_down"), sem("first_ready"))
        rank_counted, offs_ready, slot_ready, slotT, chain = (
            sem("rank_counted"), sem("offs_ready"), sem("slot_ready"), sem("slotT"), sem("chain"))
        parts_ready, pool_turn, second_ready = sem("parts_ready"), sem("pool_turn"), sem("second_ready")
        adds_landed = sem("adds_landed")
        act_turn = sem("act_turn")
        table_done = [sem(f"table_done{i}") for i in range(2)]
        first_done = [sem(f"first_done{i}") for i in range(2)]
        onehot_ready, idx_summed, idx_ready = sem("onehot_ready"), sem("idx_summed"), sem("idx_ready")
        gathered = [sem(f"gathered{i}") for i in range(4)]
        idx_kept, parts_of_ready = sem("idx_kept"), sem("parts_of_ready")
        scattered = [sem(f"scattered{i}") for i in range(2)]
        xin_T, x_hi_ready, x_lo_ready = sem("xin_T"), sem("x_hi_ready"), sem("x_lo_ready")
        w_hi_ready, w_lo_ready = sem("w_hi_ready"), sem("w_lo_ready")
        gu_ready, silu_ready, act_ready = sem("gu_ready"), sem("silu_ready"), sem("act_ready")
        down_ready, y_read, y_done = sem("down_ready"), sem("y_read"), sem("y_done")

        def loads(s, e, slots=2):
            return e // slots * s + s

        UNROLL = 4
        TURNS = (E - 4) // UNROLL

        sh_bank = [bank[1], bank[7]]
        rows_bank = [bank[0], bank[6], bank[2], bank[3]]

        def shared_behind(n, finish, start):
            if n in IN_STEPS:
                start(IN_STEPS.index(n))
            if n in OUT_STEPS:
                finish(OUT_STEPS.index(n))

        def shared_slot(n, finish, start):
            if len(OUT_STEPS) + n < B:
                finish(len(OUT_STEPS) + n)
            if len(IN_STEPS) + n < B:
                start(len(IN_STEPS) + n)

        block = ctx.enter_context(nc.Block())

        @block.sync
        def _(sp):
            sp.dma_start(fsT_sb[:], fsT).then_inc(ld_fs, 16)
            for g in range(4):
                sp.dma_start(xT_sb[:, 4 * g:4 * g + 4, :], xT[:, 4 * g:4 * g + 4, :]).then_inc(ld_x[g], 16)
            sp.dma_start(cf_sb[:, C_FIRST:], cf[:, C_FIRST:]).then_inc(ld_cf, 16)
            sp.dma_start(cb_sb[:], cb).then_inc(ld_cb, 16)
            sp.dma_start(sh_sb[:], shw).then_inc(ld_sh, 16)
            for e in range(2):
                sp.dma_start(wgu_sb[e][:], wgu[e]).then_inc(ld_wgu[e], 16)
                sp.dma_start(wd_sb[e][:], wd[e]).then_inc(ld_wd[e], 16)
            for e in range(2, 4):
                sp.dma_start(wgu_sb[e][:], wgu[e]).then_inc(ld_wgu[e], 16)
            sp.dma_start(db_sb[:], down_b.partition_broadcast(P)).then_inc(ld_db, 16)
            sp.wait_ge(hrow_ready, 4)
            sp.wait_ge(hscore_ready, 1)
            trows = table.rearrange("(b p) c -> p b c", p=P)
            for n in range(2):
                sp.dma_start(trows[:, 8 * n:8 * n + 8, :], hrow[:, 8 * n:8 * n + 8, :]).then_inc(table_done[n], 16)
            orows = out.rearrange("b p c -> p b c")
            for n in range(2):
                sp.wait_ge(first_ready, 8 * n + 8)
                sp.dma_start(orows[:, 8 * n:8 * n + 8, :], first[:, 8 * n:8 * n + 8, :]).then_inc(first_done[n], 16)

            def load_gu(e, p):
                sp.wait_ge(act_ready, e * FC - 3 * FC)
                sp.dma_start(wgu_sb[p][:], wgu[bass.ds(e, 1)].rearrange("o p c -> (o p) c")).then_inc(ld_wgu[p], 16)

            def load_d(e, p):
                sp.wait_ge(down_ready, e - 1)
                sp.dma_start(wd_sb[p][:], wd[bass.ds(e, 1)].rearrange("o p c d -> (o p) c d")).then_inc(ld_wd[p], 16)

            with sp.Fori(0, TURNS) as i:
                for u in range(UNROLL):
                    load_gu(i * UNROLL + (4 + u), u)
                    load_d(i * UNROLL + (2 + u), u % 2)
            for e in range(E - 2, E):
                load_d(e, e % 2)
            for s in scattered:
                sp.wait_ge(s, 16 * CT * E // 2)

        @block.tensor
        def _(pe):
            def keep_warm(n, to=bank[7]):
                for _ in range(n):
                    pe.matmul(to[:, :], nc.const_aps.tensor(1.0, [P, P], BF16),
                              nc.const_aps.tensor(1.0, [P, 512], BF16), start=True, stop=True)

            keep_warm(WARM)

            def low_rank(g):
                for n in range(4):
                    f = fsT_sb[:, 4 * g + n, :]
                    mm = pe.matmul(bank[g][:, n * P:(n + 1) * P], f, f, start=True, stop=True)
                mm.then_inc(lowrank_ready, 1)

            def project(g):
                pe.wait_ge(weff_ready, g + 1)
                pe.wait_ge(ld_x[g], 16)
                for n in range(4):
                    mm = pe.matmul(bank[4 + g][:, n * P:(n + 1) * P], weff[:, 4 * g + n, :],
                                   xT_sb[:, 4 * g + n, :], start=True, stop=True)
                mm.then_inc(y_ready, 1)

            def logits(g):
                for k in range(g * 4 // HB, (g + 1) * 4 // HB):
                    pe.wait_ge(h_ready, max(HB * (k + 1), 4))
                    at = C_GATE + GATE_AT - E * k
                    mm = pe.matmul(bank[4][:, 0:CH], cf_sb[:, at:at + P], hT[:, k * CH:(k + 1) * CH],
                                   start=(k == 0), stop=(k == K - 1))
                if g == 3:
                    mm.then_inc(logits_ready, 1)

            def h_rows(g):
                for b in range(4 * g, 4 * g + 4):
                    tr = pe.transpose(rows_bank[g][:, b % 4 * P:(b % 4 + 1) * P], hT[:, b * P:(b + 1) * P], ident)
                tr.then_inc(hrow_T, 1)

            pe.wait_ge(ld_fs, 16)
            low_rank(0)
            low_rank(1)
            project(0)
            low_rank(2)
            project(1)
            low_rank(3)
            project(2)
            pe.wait_ge(ld_cf, 16)
            logits(0)
            project(3)
            h_rows(0)
            for g in range(1, 4):
                logits(g)
            for g in ROWS_ORDER:
                h_rows(g)

            def shared_in(t):
                if t > 1:
                    pe.wait_ge(sh_up_ready, t - 1)
                for c in range(2 * SC):
                    mm = pe.matmul(sh_bank[t % 2][:, c * P:(c + 1) * P], sh_sb[:, c * P:(c + 1) * P],
                                   hT[:, t * P:(t + 1) * P], start=True, stop=True)
                mm.then_inc(sh_gu, 1)

            def shared_out(t, chunks=range(SC)):
                if 0 in chunks:
                    if t:
                        pe.wait_ge(first_ready, t)
                    else:
                        pe.wait_ge(hrow_ready, 2)
                    pe.matmul(bank[2][:, 0:P], xT_sb[:, t, :], ident, start=True, stop=False)
                    pe.wait_ge(sh_act_ready, t + 1)
                for c in chunks:
                    mm = pe.matmul(bank[2][:, 0:P], sh_act[t % 2][:, c * P:(c + 1) * P],
                                   sh_sb[:, S_D + c * P:S_D + (c + 1) * P], start=False, stop=(c == SC - 1))
                if SC - 1 in chunks:
                    mm.then_inc(sh_down, 1)

            def sum_counts(n):
                pe.wait_ge(counted, n + 1)
                if n >= len(UPPER):
                    pe.wait_ge(higher_ready, 1)
                    pe.matmul(bank[0][:, 0:3], ones, cnt[:, 3:4].broadcast_to([P, 3]), start=True, stop=False)
                pe.matmul(bank[0][:, 0:2], ones, cnt[:, 0:2], start=n < len(UPPER), stop=n < len(UPPER))
                pe.wait_ge(counted_act, n + 1)
                pe.matmul(bank[0][:, 2:3], half, cnt[:, 2:3], start=n < len(UPPER), stop=True).then_inc(summed, 1)

            pe.wait_ge(ld_cb, 16)
            pe.wait_ge(ld_sh, 16)
            pe.wait_ge(hrow_ready, 1)
            pe.wait_ge(score_ready, 1)
            for h in range(HB):
                tr = pe.transpose(bank[5][:, h * P:(h + 1) * P], score[:, h * P:(h + 1) * P], ident)
            tr.then_inc(scoreT, 1)
            keep_warm(2)
            for n in range(STEPS):
                sum_counts(n)
                if n - 1 in OUT_STEPS:
                    shared_out(OUT_STEPS.index(n - 1), [SC - 1])
                shared_behind(n, lambda t: shared_out(t, range(SC - 1)), shared_in)
            shared_out(len(OUT_STEPS) - 1, [SC - 1])
            slot_n = iter(range(SLOTS))

            def shared_next():
                shared_slot(next(slot_n), shared_out, shared_in)

            pe.wait_ge(rank_counted, 1)
            pe.matmul(bank[0][:, 8:10], lower, rank_cnt[:, 1:3], start=True, stop=False)
            pe.matmul(bank[0][:, 8:10], ones, rank_cnt[:, 0:2], start=False, stop=True).then_inc(offs_ready, 1)
            shared_next()
            pe.wait_ge(hrow_ready, 4)
            pe.wait_ge(slot_ready, 1)
            for h in range(HB):
                tr = pe.transpose(bank[3][:, h * P:(h + 1) * P], slot[:, h * P:(h + 1) * P], ident)
            tr.then_inc(slotT, 1)
            keep_warm(6, bank[6])

            def sum_indices(e, p, ahead):
                pe.wait_ge(onehot_ready, e + 1)
                pe.wait_ge(parts_of_ready, e + 1)
                if ahead:
                    pe.wait_ge(idx_ready, e)
                for b in range(B):
                    mm = pe.matmul(bank[0][:, 0:4 * CT], onehot[p][:, :, b],
                                   parts_of[p][:, :, b],
                                   start=(b == 0), stop=(b == B - 1))
                mm.then_inc(idx_summed, 1)

            def transpose_rows(e, slot, ahead):
                pe.wait_ge(gathered[slot], loads(16 * CT, e, 4))
                if ahead:
                    pe.wait_ge(x_lo_ready, e)
                for c in range(CT):
                    tr = pe.transpose(bank[3][:, c * P:(c + 1) * P], rows[slot][:, c, 0:P], ident)
                tr.then_inc(xin_T, 1)

            def gate_up(e, p, ahead):
                pe.wait_ge(x_lo_ready, e + 1)
                pe.wait_ge(w_lo_ready, e * 2 + 2)
                for f in range(FC):
                    if ahead:
                        pe.wait_ge(act_ready, e * FC + (f + 1 - FC))
                    for n in range(2):
                        w = slice(n * F + f * P, n * F + (f + 1) * P)
                        to = bank[4 + f][:, n * CAP:(n + 1) * CAP]
                        pe.matmul(to, w_hi[p][:, w], x_hi[p][:], start=True, stop=False)
                        pe.matmul(to, w_hi[p][:, w], x_lo[p][:], start=False, stop=False)
                        mm = pe.matmul(to, w_lo[p][:, w], x_hi[p][:], start=False, stop=True)
                    mm.then_inc(gu_ready, 1)

            def down(e, p, ahead, by_tile=False):
                pe.wait_ge(ld_wd[p], loads(16, e))
                if ahead:
                    pe.wait_ge(y_read, e)
                for f in range(FC):
                    pe.wait_ge(act_ready, e * FC + (f + 1))
                    for c in range(CT):
                        mm = pe.matmul(down_banks[:, c, 0:P], act_sb[p][:, f, c * P:(c + 1) * P],
                                       wd_sb[p][:, f, :], start=(f == 0), stop=(f == FC - 1))
                        if by_tile and f == FC - 1:
                            mm.then_inc(down_ready, 1)
                if not by_tile:
                    mm.then_inc(down_ready, 1)

            def expert(e, p, next_slot):
                transpose_rows(e + 1, next_slot, True)
                gate_up(e, p, True)
                sum_indices(e + 3, 1 - p, True)
                down(e, p, True)

            sum_indices(0, 0, False)
            shared_next()
            sum_indices(1, 1, True)
            sum_indices(2, 0, True)
            shared_next()
            keep_warm(2, bank[6])
            transpose_rows(0, 0, False)
            shared_next()
            pe.wait_ge(sh_up_ready, B)
            gate_up(0, 0, False)
            transpose_rows(1, 1, True)
            sum_indices(3, 1, True)
            pe.wait_ge(first_ready, B)
            down(0, 0, False)
            with pe.Fori(0, TURNS) as i:
                for u in range(UNROLL):
                    expert(i * UNROLL + (1 + u), (1 + u) % 2, (2 + u) % 4)
            for e in range(E - 3, E):
                if e + 1 < E:
                    transpose_rows(e + 1, (e + 1) % 4, True)
                gate_up(e, e % 2, True)
                down(e, e % 2, True, e == E - 1)

        @block.scalar
        def _(act):
            act.dma_start(cf_sb[:, 0:C_FIRST], cf[:, 0:C_FIRST]).then_inc(ld_wt, 16)
            act.wait_ge(warm_ready, 1)
            act.activation(spare[:, 0:1], warm[:, 0:1], ACT.Gelu)
            act.wait_ge(bias_ready, 1)
            for b in range(B):
                if b % 4 == 0:
                    act.wait_ge(y_ready, b // 4 + 1)
                act.activation(hT[:, b * P:(b + 1) * P], bank[4 + b // 4][:, b % 4 * P:(b % 4 + 1) * P],
                               ACT.Gelu, bias=biasT[:, b:b + 1]).then_inc(h_ready, 1)

            def upper_weights(e, n, p, slot, ahead):
                if n == 0:
                    act.wait_ge(ld_wgu[slot], loads(16, e, 4))
                    if ahead:
                        act.wait_ge(gu_ready, e * FC - FC)
                act.activation(w_hi[p][:, n * F:(n + 1) * F], wgu_sb[slot][:, n * F:(n + 1) * F], ACT.Copy
                               ).then_inc(w_hi_ready, 1)

            upper_weights(0, 0, 0, 0, False)
            act.wait_ge(logits_ready, 1)
            act.activation(score[:], bank[4][:, 0:CH], ACT.Sigmoid).then_inc(score_ready, 1)
            act.wait_ge(score_ready, 1)

            def second_part():
                act.wait_ge(second_ready, 1)
                act.activation(parts[:, 1, 2], second[:], ACT.Copy, scale=token).then_inc(parts_ready, 1)
                act.activation(parts[:, 0, 2], second[:], ACT.Copy, scale=token_neg).then_inc(parts_ready, 1)

            def count_third(n):
                act.wait_ge(cand_ready, n + 1)
                if n:
                    act.wait_ge(summed, n)
                if n == 1:
                    act.wait_ge(coarse_ready, 1)
                if n == len(UPPER):
                    act.wait_ge(fine_ready, 1)
                with nc.allow_low_precision(reason="integers up to 256"):
                    data = (coarse[:] if n else halves[:, :, 1]) if n < len(UPPER) else fine[:]
                    act.activation(signs[:], data, ACT.Sign,
                                   bias=cand[:, 2:3], accum_out=cnt[:, 2:3]).then_inc(counted_act, 1)

            def shared_read(t):
                act.wait_ge(sh_gu, t + 1)
                if t > 1:
                    act.wait_ge(sh_act_ready, t - 1)
                act.activation(sh_silu[t % 2][:], sh_bank[t % 2][:, 0:SH], ACT.Silu)
                act.activation(sh_up[t % 2][:], sh_bank[t % 2][:, SH:2 * SH], ACT.Copy).then_inc(sh_up_ready, 1)

            def shared_y(t):
                act.wait_ge(sh_down, t + 1)
                act.activation(first[:, t, :], bank[2][:, 0:P], ACT.Copy).then_inc(first_ready, 1)

            count_third(0)
            act.activation(coarse[:], halves[:, :, 1], ACT.Copy).then_inc(coarse_ready, 1)
            act.activation(spare[:, 1:2], warm[:, 0:1], ACT.Silu)
            for n in range(1, STEPS):
                count_third(n)
                shared_behind(n - 1, shared_y, shared_read)
                if n == UPPER_STEP:
                    upper_weights(0, 1, 0, 0, False)
                if n == 1:
                    act.wait_ge(scoreT, 1)
                    act.activation(hrow[:, :, P:ROW].rearrange("p (k h) e -> p h k e", h=HB),
                                   bank[5][:, 0:CH].rearrange("p (h k e) -> p h k e", h=HB, k=K), ACT.Copy
                                   ).then_inc(hscore_ready, 1)

            def copy_parts(e, p, ahead):
                if ahead:
                    act.wait_ge(idx_summed, e - 1)
                    act.sem_inc(act_turn, 1)
                act.activation(parts_of[p][:], parts[:, :, :, bass.ds(e, 1), :].rearrange(
                    "p n q o b -> p (n q o) b"), ACT.Copy).then_inc(parts_of_ready, 1)

            shared_behind(STEPS - 1, shared_y, shared_read)
            for n in range(2):
                upper_weights(1, n, 1, 1, False)
            for n in range(SLOTS - 1):
                if n == 1:
                    second_part()
                    act.wait_ge(parts_ready, 6)
                    copy_parts(0, 0, False)
                    copy_parts(1, 1, False)
                if n == 2:
                    copy_parts(2, 0, True)
                shared_slot(n, shared_y, shared_read)

            def read_rows(e, p, slot, ahead):
                act.wait_ge(gathered[slot], loads(16 * CT, e, 4))
                act.activation(weight[slot][:],
                               rows[slot][:, :, bass.ds(P + e, 1)].rearrange("p c o -> p (c o)"), ACT.Copy)
                act.wait_ge(xin_T, e + 1)
                if ahead:
                    act.wait_ge(gu_ready, e * FC - FC)
                act.activation(x_hi[p][:], bank[3][:, 0:CAP], ACT.Copy).then_inc(x_hi_ready, 1)

            def silus(e, p, slot, ahead):
                for f in range(FC):
                    act.wait_ge(gu_ready, e * FC + (f + 1))
                    if ahead:
                        act.wait_ge(act_ready, e * FC + (f + 1 - FC))
                    act.activation(silu[:, f, :], bank[4 + f][:, 0:CAP], ACT.Silu,
                                   bias=wgu_sb[slot][:, G_GB + f:G_GB + f + 1]).then_inc(silu_ready, 1)

            def keep_indices(e, p, slot, ahead):
                act.wait_ge(idx_ready, e + 1)
                if ahead:
                    act.wait_ge(adds_landed, e)
                act.activation(idx_s[p][:], idx_g[slot][:], ACT.Copy).then_inc(idx_kept, 1)

            def scaled(e, p, slot):
                act.wait_ge(y_read, e + 1)
                for c in range(CT):
                    y = act.activation(y_sb[p][:, c, :], y_raw[:, c, :], ACT.Copy,
                                       scale=weight[slot][:, c:c + 1])
                y.then_inc(y_done, 1)

            read_rows(0, 0, 0, False)
            shared_slot(SLOTS - 1, shared_y, shared_read)
            silus(0, 0, 0, False)
            copy_parts(3, 1, True)
            read_rows(1, 1, 1, False)
            keep_indices(0, 0, 0, False)
            upper_weights(2, 0, 0, 2, True)
            read_rows(2, 0, 2, True)
            scaled(0, 0, 0)
            with act.Fori(0, TURNS) as i:
                for u in range(UNROLL):
                    e = i * UNROLL + (1 + u)
                    copy_parts(e + 3, u % 2, True)
                    silus(e, 1 - u % 2, (1 + u) % 4, True)
                    keep_indices(e, 1 - u % 2, (1 + u) % 4, True)
                    upper_weights(e + 1, 1, u % 2, (2 + u) % 4, True)
                    upper_weights(e + 2, 0, 1 - u % 2, (3 + u) % 4, True)
                    read_rows(e + 2, 1 - u % 2, (3 + u) % 4, True)
                    scaled(e, 1 - u % 2, (1 + u) % 4)
            for e in range(E - 3, E):
                silus(e, e % 2, e % 4, True)
                keep_indices(e, e % 2, e % 4, True)
                if e + 1 < E:
                    upper_weights(e + 1, 1, (e + 1) % 2, (e + 1) % 4, True)
                if e + 2 < E:
                    upper_weights(e + 2, 0, e % 2, (e + 2) % 4, True)
                    read_rows(e + 2, e % 2, (e + 2) % 4, True)
                if e + 1 < E:
                    scaled(e, e % 2, e % 4)
            for c in range(CT):
                act.wait_ge(y_read, E + c)
                act.activation(y_sb[1][:, c, :], y_raw[:, c, :], ACT.Copy, scale=weight[3][:, c:c + 1]
                               ).then_inc(y_done, 1)

        @block.gpsimd
        def _(pool):
            def shared_mul(t, p, ahead):
                pool.wait_ge(sh_up_ready, t + 1)
                if ahead:
                    pool.wait_ge(sh_down, t - 1)
                pool.tensor_tensor(sh_act[p][:], sh_silu[p][:], sh_up[p][:], ALU.mult).then_inc(sh_act_ready, 1)

            pool.memset(parts[:, 1, 0:2], 0.0)
            pool.wait_ge(ld_cb, 16)
            pool.tensor_copy(parts[:, 0, 1], block_at).then_inc(parts_ready, 1)
            for t in range(2):
                shared_mul(t, t, False)
            with pool.Fori(1, 6) as i:
                for u in range(2):
                    shared_mul(i * 2 + u, u, True)
            shared_mul(B - 4, 0, True)
            pool.wait_ge(second_ready, 1)
            pool.tensor_tensor(parts[:, 1, 3], second[:], block_at, ALU.mult).then_inc(parts_ready, 1)
            pool.tensor_tensor(parts[:, 0, 3], second[:], block_neg, ALU.mult).then_inc(parts_ready, 1)
            shared_mul(B - 3, 1, True)

            def gather(e, slot, ahead):
                pool.wait_ge(idx_ready, e + 1)
                if ahead:
                    pool.wait_ge(x_hi_ready, e - 3)
                pool.sem_inc(pool_turn, 1)
                for c in range(CT):
                    pool.indirect_dma_start(rows[slot][:, c, :], None, table,
                                            bass.IndirectOffsetOnAxis(ap=idx_g[slot][:, c:c + 1], axis=0)
                                            ).then_inc(gathered[slot], 16)

            def add_rows(p, c):
                pool.indirect_dma_start(out.rearrange("b p c -> (b p) c"),
                                        bass.IndirectOffsetOnAxis(ap=idx_s[p][:, c:c + 1], axis=0),
                                        y_sb[p][:, c, :], None, compute_op=ALU.add).then_inc(scattered[p], 16)

            def scatter(e, p):
                pool.wait_ge(y_done, e + 1)
                pool.wait_ge(scattered[1 - p], (e + 1) // 2 * (16 * CT))
                pool.sem_inc(adds_landed, 1)
                for c in range(CT):
                    add_rows(p, c)

            for n in range(2):
                pool.wait_ge(table_done[n], 16)
            gather(0, 0, False)
            shared_mul(B - 2, 0, True)
            gather(1, 1, False)
            shared_mul(B - 1, 1, True)
            gather(2, 2, False)
            gather(3, 3, False)
            for n in range(2):
                pool.wait_ge(first_done[n], 16)
            scatter(0, 0)
            with pool.Fori(0, TURNS) as i:
                for u in range(UNROLL):
                    gather(i * UNROLL + (4 + u), u, True)
                    scatter(i * UNROLL + (1 + u), (1 + u) % 2)
            for e in range(E - 3, E - 1):
                scatter(e, e % 2)
            pool.wait_ge(scattered[0], E // 2 * (16 * CT))
            for c in range(CT):
                pool.wait_ge(y_done, E + c)
                add_rows(1, c)

        @block.vector
        def _(dve):
            linked = [0]

            def link(ins):
                linked[0] += 1
                ins.then_inc(chain, 1)
                dve.wait_ge(chain, linked[0])

            dve.memset(warm[:], 0.0).then_inc(warm_ready, 1)
            dve.memset(zeros[:], 0.0)
            dve.memset(rank_cnt[:], 0.0)
            dve.wait_ge(ld_wt, 16)
            dve.tensor_scalar(biasT[:], cf_sb[:, C_COND:C_COND + B], cf_sb[:, C_FCB:C_FCB + 1], None, ALU.add
                              ).then_inc(bias_ready, 1)
            for g in range(4):
                dve.wait_ge(lowrank_ready, g + 1)
                dve.scalar_tensor_tensor(weff[:, 4 * g:4 * g + 4, :],
                                         bank[g][:, :].rearrange("p (b o) -> p b o", b=4), 1.0 / (P * R),
                                         WT[:, None, :].broadcast_to([P, 4, P]), ALU.mult, ALU.add
                                         ).then_inc(weff_ready, 1)
            dve.wait_ge(ld_cf, 16)
            link(dve.tensor_copy(cand[:], cf_sb[:, C_NEXT:C_NEXT + 3]))
            dve.engine_nop().then_inc(cand_ready, 1)
            dve.wait_ge(ld_cb, 16)
            dve.tensor_scalar(parts[:, 0, 0], block_at, 0.0, token, ALU.mult, ALU.add).then_inc(parts_ready, 1)

            def copy_rows(g, blocks):
                dve.wait_ge(hrow_T, 2 + ROWS_ORDER.index(g) if g else 1)
                return dve.tensor_copy(hrow[:, 4 * g + blocks.start:4 * g + blocks.stop, 0:P],
                                       rows_bank[g][:, blocks.start * P:blocks.stop * P].rearrange(
                                           "p (b o) -> p b o", o=P))

            copy_rows(0, slice(0, 4)).then_inc(hrow_ready, 1)

            def lower_weights(e, n, p, slot):
                dve.wait_ge(w_hi_ready, e * 2 + (n + 1))
                dve.tensor_tensor(w_lo[p][:, n * F:(n + 1) * F], wgu_sb[slot][:, n * F:(n + 1) * F],
                                  w_hi[p][:, n * F:(n + 1) * F], ALU.subtract).then_inc(w_lo_ready, 1)

            dve.wait_ge(score_ready, 1)
            for n in range(STEPS):
                upper = n < len(UPPER)
                data = (coarse[:] if n else halves[:, :, 1]) if upper else fine[:]
                first_step = n in (0, len(UPPER))
                last_step = n in (len(UPPER) - 1, STEPS - 1)
                if n == 1:
                    dve.wait_ge(coarse_ready, 1)
                if n == len(UPPER):
                    dve.tensor_scalar(higher[:], coarse[:], coarse_at[:], None, ALU.is_gt, ALU.add,
                                      accum_out=cnt[:, 3:4]).then_inc(higher_ready, 1)
                for j in range(2):
                    c = dve.tensor_scalar(hits[:, j, :], data, cand[:, j:j + 1], -CH / 2, ALU.is_ge, ALU.add,
                                          accum_out=cnt[:, j:j + 1])
                c.then_inc(counted, 1)
                if n == len(UPPER) + 1:
                    dve.tensor_scalar(same[:], coarse[:], coarse_at[:], None, ALU.is_equal)
                if not first_step:
                    link(dve.tensor_scalar(place4[:], place[:], 4.0, None, ALU.mult))
                if n in ROWS_STEPS:
                    m = ROWS_STEPS.index(n)
                    part = copy_rows(ROWS_ORDER[m // 2], slice(m % 2 * 2, m % 2 * 2 + 2))
                    if m % 2:
                        part.then_inc(hrow_ready, 1)
                if n in LOWER_STEPS:
                    m = LOWER_STEPS.index(n)
                    w = slice(m * F // 2, (m + 1) * F // 2)
                    dve.wait_ge(w_hi_ready, m // 2 + 1)
                    part = dve.tensor_tensor(w_lo[0][:, w], wgu_sb[0][:, w], w_hi[0][:, w], ALU.subtract)
                    if m % 2:
                        part.then_inc(w_lo_ready, 1)
                dve.wait_ge(summed, n + 1)
                link(dve.tensor_scalar(passed[:], bank[0][:, 0:3], float(CAP - T // 2),
                                       0.0 if first_step else place4[:], ALU.is_ge, ALU.add,
                                       accum_out=place[:]))
                if not last_step:
                    unit = C_UNIT + 3 * n
                    nxt = C_NEXT + 3 * (n + 1)
                    dve.scalar_tensor_tensor(cand[:], cf_sb[:, unit:unit + 3], place[:],
                                             cf_sb[:, nxt:nxt + 3], ALU.mult, ALU.add).then_inc(cand_ready, 1)
                    dve.wait_ge(cand_ready, n + 2)
                elif upper:
                    dve.scalar_tensor_tensor(fine[:], coarse[:], place[:], halves[:, :, 0], ALU.is_equal,
                                             ALU.mult).then_inc(fine_ready, 1)
                    dve.tensor_copy(coarse_at[:], place[:])
                    nxt = C_NEXT + 3 * (n + 1)
                    dve.tensor_copy(cand[:], cf_sb[:, nxt:nxt + 3]).then_inc(cand_ready, 1)
                    dve.wait_ge(cand_ready, n + 2)
            dve.scalar_tensor_tensor(above[:], fine[:], place[:], higher[:], ALU.is_gt, ALU.add)
            link(dve.scalar_tensor_tensor(equal[:], fine[:], place[:], same[:], ALU.is_equal, ALU.mult))
            dve.tensor_tensor_scan(ranks[:, 0, :], above[:], zeros[:], 0.0, ALU.add, ALU.add)
            link(dve.tensor_tensor_scan(ranks[:, 1, :], equal[:], zeros[:], 0.0, ALU.add, ALU.add))
            dve.tensor_copy(rank_cnt[:, 1:3], ranks[:, :, CH - 1]).then_inc(rank_counted, 1)
            dve.wait_ge(offs_ready, 1)
            dve.scalar_tensor_tensor(above[:], ranks[:, 0, :], bank[0][:, 8:9], above[:], ALU.add, ALU.mult)
            link(dve.scalar_tensor_tensor(equal[:], ranks[:, 1, :], bank[0][:, 9:10], equal[:], ALU.add, ALU.mult))
            dve.tensor_tensor(slot[:], above[:], equal[:], ALU.add).then_inc(slot_ready, 1)
            lower_weights(1, 0, 1, 1)
            dve.wait_ge(slotT, 1)
            at = bank[3][:, 0:CH].rearrange("p (b e) -> p e b", e=E)
            dve.tensor_scalar(second[:], at, float(P), None, ALU.is_gt).then_inc(second_ready, 1)
            dve.wait_ge(second_ready, 1)
            link(dve.scalar_tensor_tensor(row_of[:], second[:], -float(P), at, ALU.mult, ALU.add))

            def one_hot(e, p, ahead):
                if ahead:
                    dve.wait_ge(idx_summed, e - 1)
                dve.tensor_tensor(onehot[p][:], iota, row_of[:, bass.ds(e, 1), :].broadcast_to([P, P, B]),
                                  ALU.is_equal).then_inc(onehot_ready, 1)

            def indices(e, slot, ahead):
                dve.wait_ge(idx_summed, e + 1)
                if ahead:
                    dve.wait_ge(gathered[slot], loads(16 * CT, e - 4, 4))
                    dve.wait_ge(idx_kept, e - 3)
                pair = bank[0][:, 0:4 * CT].rearrange("p (n q) -> p n q", q=4)
                with nc.allow_low_precision(reason="token numbers"):
                    dve.tensor_reduce(idx_g[slot][:], pair, AX_X, ALU.add).then_inc(idx_ready, 1)

            def gated(e, p, slot):
                for f in range(FC):
                    dve.wait_ge(silu_ready, e * FC + (f + 1))
                    dve.scalar_tensor_tensor(act_sb[p][:, f, :], bank[4 + f][:, CAP:2 * CAP],
                                             wgu_sb[slot][:, G_UB + f:G_UB + f + 1], silu[:, f, :],
                                             ALU.add, ALU.mult).then_inc(act_ready, 1)

            def lower_rows(e, p):
                dve.wait_ge(x_hi_ready, e + 1)
                dve.tensor_tensor(x_lo[p][:], bank[3][:, 0:CAP], x_hi[p][:], ALU.subtract).then_inc(x_lo_ready, 1)

            def biased(e, ahead):
                dve.wait_ge(down_ready, e + 1)
                if ahead:
                    dve.wait_ge(y_done, e)
                dve.tensor_tensor(y_raw[:], down_banks[:, :, 0:P],
                                  db_sb[:, bass.ds(e, 1), :].broadcast_to([P, CT, P]), ALU.add
                                  ).then_inc(y_read, 1)

            one_hot(0, 0, False)
            lower_weights(1, 1, 1, 1)
            indices(0, 0, False)
            one_hot(1, 1, False)
            one_hot(2, 0, True)
            indices(1, 1, False)
            one_hot(3, 1, True)
            indices(2, 2, False)
            dve.wait_ge(ld_db, 16)
            lower_rows(0, 0)
            gated(0, 0, 0)
            indices(3, 3, False)
            lower_rows(1, 1)
            biased(0, False)
            with dve.Fori(0, TURNS) as i:
                for u in range(UNROLL):
                    e = i * UNROLL + (1 + u)
                    p = (1 + u) % 2
                    one_hot(e + 3, 1 - p, True)
                    lower_rows(e + 1, 1 - p)
                    lower_weights(e + 1, 0, 1 - p, (2 + u) % 4)
                    gated(e, p, (1 + u) % 4)
                    lower_weights(e + 1, 1, 1 - p, (2 + u) % 4)
                    indices(e + 3, u, True)
                    biased(e, True)
            for e in range(E - 3, E):
                if e + 1 < E:
                    lower_rows(e + 1, 1 - e % 2)
                    lower_weights(e + 1, 0, 1 - e % 2, (e + 1) % 4)
                gated(e, e % 2, e % 4)
                if e + 1 < E:
                    lower_weights(e + 1, 1, 1 - e % 2, (e + 1) % 4)
                if e + 1 < E:
                    biased(e, True)
            dve.wait_ge(y_done, E - 1)
            for c in range(CT):
                dve.wait_ge(down_ready, E + c)
                dve.tensor_tensor(y_raw[:, c, :], down_banks[:, c, 0:P], db_sb[:, E - 1, :], ALU.add
                                  ).then_inc(y_read, 1)


def kernel(x, fside_Bx1x1024x16_0, cond_1024, L0_cond_W, L0_cond_fc_bias, L0_ffn_gate_w, L0_ffn_up_w, L0_ffn_up_b,
           L0_ffn_gw, L0_ffn_gb, L0_ffn_down_w, L0_ffn_down_b, L0_ffn_sh_gate_w, L0_ffn_sh_up_w, L0_ffn_sh_down_w):
    import ml_dtypes
    import numpy as np
    import concourse.bacc as bacc
    from concourse.bass_utils import run_bass_kernel_spmd

    f32 = np.float32
    p = np.arange(P)
    cf = np.zeros((P, C_N), f32)
    cf[:, C_WT:C_WT + P] = np.transpose(L0_cond_W)
    cf[:, C_COND:C_COND + B] = np.transpose(cond_1024)
    cf[:, C_FCB] = L0_cond_fc_bias
    cf[:, C_GATE + GATE_AT:C_GATE + GATE_AT + E] = np.transpose(L0_ffn_gate_w)
    cf[:, C_ID:C_ID + P] = np.eye(P)
    cf[:, C_J] = p
    cf[:, C_J + 1] = -p
    for n in range(STEPS):
        unit = (UPPER + LOWER)[n]
        cf[:, C_UNIT + 3 * n:C_UNIT + 3 * n + 3] = unit, unit, -unit
        cf[:, C_NEXT + 3 * n:C_NEXT + 3 * n + 3] = unit, 2 * unit, 0.5 - 3 * unit
    cb = np.zeros((P, B_N), f32)
    same = p[:, None] % E == p[None, :] % E
    cb[:, B_ONES:B_ONES + P] = same
    cb[:, B_HALF:B_HALF + P] = 0.5 * same
    cb[:, B_LOW:B_LOW + P] = same & (p[:, None] // E < p[None, :] // E)
    cb[:, B_IOTA:B_IOTA + P * B] = np.repeat(p + 1, B)
    cb[:, B_BLK:B_BLK + E * B] = np.tile((P * np.arange(B)).reshape(K, HB).T.ravel(), E)
    cb[:, B_NEG:B_NEG + E * B] = -cb[:, B_BLK:B_BLK + E * B]
    cb = cb.astype(ml_dtypes.bfloat16)

    def down_layout(w):
        h = w.shape[-1]
        v = np.swapaxes(np.asarray(w), -1, -2)
        v = v.reshape(v.shape[:-2] + (h // P, P, P))
        return np.ascontiguousarray(np.moveaxis(v, -3, -2))

    def bias_layout(v):
        return np.moveaxis(np.asarray(v).reshape(E, FC, P), 1, 2)

    arrays = {
        "xT": np.ascontiguousarray(np.transpose(x, (2, 0, 1))),
        "fsT": np.ascontiguousarray(np.transpose(np.asarray(fside_Bx1x1024x16_0)[:, 0], (2, 0, 1))),
        "cf": cf,
        "cb": cb,
        "shw": np.concatenate([np.transpose(L0_ffn_sh_gate_w), np.transpose(L0_ffn_sh_up_w),
                               down_layout(L0_ffn_sh_down_w).reshape(P, SH)], axis=1),
        "wgu": np.concatenate([np.swapaxes(np.asarray(L0_ffn_gw), 1, 2), np.swapaxes(np.asarray(L0_ffn_up_w), 1, 2),
                               bias_layout(L0_ffn_gb), bias_layout(L0_ffn_up_b)], axis=2),
        "wd": down_layout(L0_ffn_down_w),
        "down_b": np.ascontiguousarray(L0_ffn_down_b),
    }
    nc = bacc.Bacc("TRN2", target_bir_lowering=False, num_devices=1)
    args = [nc.dram_tensor(f"in_{n}", a.shape, mybir.dt.from_np(a.dtype), kind="ExternalInput").ap()
            for n, a in arrays.items()]
    out = nc.dram_tensor("out_0", (B, P, P), F32, kind="ExternalOutput").ap()
    moe_program(nc, *args, out)
    r = run_bass_kernel_spmd(nc, [{f"in_{n}": a for n, a in arrays.items()}], core_ids=[0])
    return r.results[0]["out_0"]
```
